# Optimizing a Trainium2 kernel written in Bass

```python
import numpy as np
import jax
import jax.numpy as jnp

def _softmax(x, axis=-1):
    return jax.nn.softmax(x, axis=axis)

def _gelu(x):
    return jax.nn.gelu(x, approximate=True)

def _silu(x):
    return jax.nn.silu(x)

def _sigmoid(x):
    return jax.nn.sigmoid(x)

def _layernorm(x, axis=-1, eps=1e-05):
    m = jnp.mean(x, axis=axis, keepdims=True)
    v = jnp.var(x, axis=axis, keepdims=True)
    return (x - m) / jnp.sqrt(v + eps)

def _scatter_add(tgt, idx, src, axis=0):
    return tgt.at[idx].add(src)

def _segment_sum(src, seg, n):
    return jax.ops.segment_sum(src, seg, n)
kernel_name = 'mk_conv_attn_hybrid_d4_conv_nchw128_r2_2f8d71'

def setup_inputs(seed: int=0):
    np.random.seed(seed)
    _w = jnp.asarray

    def _rec_inputs():
        import jax
        import jax.numpy as jnp
        _gk = jax.random.key(seed)
        x = -0.0002928 + 1 * jax.random.normal(jax.random.fold_in(_gk, 1), (8, 64, 32, 32), jnp.float32)
        return x
    x = _rec_inputs()

    def _L0_conv_setup():
        import jax, jax.numpy as jnp
        import numpy as np
        K = 3
        STRIDE = 1
        PADDING = 1

        def _conv2d(x, w, b, stride, padding):
            out = jax.lax.conv_general_dilated(x, w, window_strides=(stride, stride), padding=[(padding, padding), (padding, padding)], dimension_numbers=('NCHW', 'OIHW', 'NCHW'))
            return out + b[None, :, None, None]

        def _grid_sample_bilinear_zeros(x, grid):
            B, C, Hin, Win = x.shape
            gx = (grid[..., 0] + 1.0) * (Win * 0.5) - 0.5
            gy = (grid[..., 1] + 1.0) * (Hin * 0.5) - 0.5
            x0f = jnp.floor(gx)
            y0f = jnp.floor(gy)
            wx1 = gx - x0f
            wy1 = gy - y0f
            x0 = x0f.astype(jnp.int32)
            y0 = y0f.astype(jnp.int32)
            xf = x.reshape(B, C, Hin * Win)

            def gather(yi, xi):
                valid = (xi >= 0) & (xi < Win) & (yi >= 0) & (yi < Hin)
                idx = jnp.clip(yi, 0, Hin - 1) * Win + jnp.clip(xi, 0, Win - 1)
                g = jax.vmap(lambda xb, ib: xb[:, ib])(xf, idx)
                return g * valid[:, None, :, :].astype(x.dtype)
            w00 = ((1.0 - wx1) * (1.0 - wy1))[:, None]
            w01 = (wx1 * (1.0 - wy1))[:, None]
            w10 = ((1.0 - wx1) * wy1)[:, None]
            w11 = (wx1 * wy1)[:, None]
            return gather(y0, x0) * w00 + gather(y0, x0 + 1) * w01 + gather(y0 + 1, x0) * w10 + gather(y0 + 1, x0 + 1) * w11
        key = jax.random.key(seed)
        k1, k2, k3 = jax.random.split(key, 3)
        B, C, O, H, W = (8, 64, 64, 32, 32)
        x = jax.random.normal(k1, (B, C, H, W), dtype=jnp.float32)
        w_off = jax.random.normal(k2, (2 * K * K, C, K, K), dtype=jnp.float32) * 0.001
        b_off = jnp.zeros((2 * K * K,), dtype=jnp.float32)
        w_main = jax.random.normal(k3, (O, C, K, K), dtype=jnp.float32) * 0.05
        b_main = jnp.zeros((O,), dtype=jnp.float32)
        return {'x': x, 'w_off': w_off, 'b_off': b_off, 'w_main': w_main, 'b_main': b_main}
    _L0_conv_all = _L0_conv_setup()
    _L0_conv_in = {k: v for k, v in _L0_conv_all.items() if k in ('w_off', 'b_off', 'w_main', 'b_main')}
    del _L0_conv_all

    def _L1_conv_setup():
        import jax, jax.numpy as jnp
        import numpy as np
        D_MODEL = 64
        D_STATE = 16
        D_CONV = 2
        EXPAND = 2
        D_INNER = EXPAND * D_MODEL
        DT_RANK = (D_MODEL + 15) // 16
        GROUPS = 4
        EPS = 1e-05

        def _causal_conv_k2(x, w, b):
            xp = jnp.pad(x, ((0, 0), (1, 0), (0, 0)))
            return xp[:, :-1] * w[:, 0] + xp[:, 1:] * w[:, 1] + b

        def _selective_scan(xc, dt, Bmat, Cmat, A, D):

            def step(h, inp):
                dt_t, B_t, C_t, x_t = inp
                dA = jnp.exp(dt_t[..., None] * A)
                dBx = dt_t[..., None] * B_t[:, None, :] * x_t[..., None]
                h = dA * h + dBx
                y = jnp.einsum('bdn,bn->bd', h, C_t)
                return (h, y)
            B_, L, Din = xc.shape
            h0 = jnp.zeros((B_, Din, A.shape[1]), dtype=xc.dtype)
            xs = (jnp.swapaxes(dt, 0, 1), jnp.swapaxes(Bmat, 0, 1), jnp.swapaxes(Cmat, 0, 1), jnp.swapaxes(xc, 0, 1))
            _, ys = jax.lax.scan(step, h0, xs)
            return jnp.swapaxes(ys, 0, 1) + xc * D

        def _mamba(x, W_in, conv_w, conv_b, W_x, W_dt, b_dt, A_log, D, W_out):
            xz = x @ W_in
            xh, z = jnp.split(xz, 2, axis=-1)
            xh = jax.nn.silu(_causal_conv_k2(xh, conv_w, conv_b))
            x_dbl = xh @ W_x
            dt_low = x_dbl[..., :DT_RANK]
            Bmat = x_dbl[..., DT_RANK:DT_RANK + D_STATE]
            Cmat = x_dbl[..., DT_RANK + D_STATE:]
            dt = jax.nn.softplus(dt_low @ W_dt + b_dt)
            A = -jnp.exp(A_log)
            y = _selective_scan(xh, dt, Bmat, Cmat, A, D)
            y = y * jax.nn.silu(z)
            return y @ W_out

        def _group_norm(x, gamma, beta):
            B_, C, H, W = x.shape
            xr = x.reshape(B_, GROUPS, -1)
            mean = xr.mean(-1, keepdims=True)
            var = xr.var(-1, keepdims=True)
            xn = ((xr - mean) * jax.lax.rsqrt(var + EPS)).reshape(B_, C, H, W)
            return xn * gamma[:, None, None] + beta[:, None, None]
        key = jax.random.key(seed)
        ks = jax.random.split(key, 12)
        s = lambda k, shape, sc=0.02: jax.random.normal(k, shape, dtype=jnp.float32) * sc
        inp = {'x_hsi': jax.random.normal(ks[0], (8, D_MODEL, 32, 32), dtype=jnp.float32), 'W_in': s(ks[1], (D_MODEL, 2 * D_INNER)), 'conv_w': s(ks[2], (D_INNER, D_CONV), 0.5), 'conv_b': s(ks[3], (D_INNER,), 0.1), 'W_x': s(ks[4], (D_INNER, DT_RANK + 2 * D_STATE)), 'W_dt': s(ks[5], (DT_RANK, D_INNER), 0.1), 'b_dt': s(ks[6], (D_INNER,), 0.1), 'A_log': jnp.log(jnp.broadcast_to(jnp.arange(1, D_STATE + 1, dtype=jnp.float32), (D_INNER, D_STATE))), 'D': jnp.ones((D_INNER,), dtype=jnp.float32), 'W_out': s(ks[7], (D_INNER, D_MODEL)), 'gn_gamma': jnp.ones((D_MODEL,), dtype=jnp.float32), 'gn_beta': jnp.zeros((D_MODEL,), dtype=jnp.float32)}
        return inp
    _L1_conv_all = _L1_conv_setup()
    _L1_conv_in = {k: v for k, v in _L1_conv_all.items() if k in ('W_in', 'conv_w', 'conv_b', 'W_x', 'W_dt', 'b_dt', 'A_log', 'D', 'W_out', 'gn_gamma', 'gn_beta')}
    del _L1_conv_all

    def _L2_attn_setup():
        import jax, jax.numpy as jnp
        import numpy as np
        B, N, D = (4, 512, 64)
        key = jax.random.key(seed)
        ks = jax.random.split(key, 4)
        scale = 1.0 / np.sqrt(D)
        return {'inputs': jax.random.normal(ks[0], (B, N, D), dtype=jnp.float32), 'Wq': jax.random.normal(ks[1], (D, D), dtype=jnp.float32) * scale, 'bq': jnp.zeros((D,), dtype=jnp.float32), 'Wk': jax.random.normal(ks[2], (D, D), dtype=jnp.float32) * scale, 'bk': jnp.zeros((D,), dtype=jnp.float32), 'Wv': jax.random.normal(ks[3], (D, D), dtype=jnp.float32) * scale, 'bv': jnp.zeros((D,), dtype=jnp.float32)}
    _L2_attn_all = _L2_attn_setup()
    _L2_attn_in = {k: v for k, v in _L2_attn_all.items() if k in ('Wq', 'bq', 'Wk', 'bk', 'Wv', 'bv')}
    del _L2_attn_all

    def _L2_ffn_setup():
        import jax, jax.numpy as jnp
        import numpy as np
        PADDED_SL = 4096
        TEMPERATURE = 1.0
        SIGMA_POW = 0.25

        def _stu_conv(phi, u, n):
            b, sl, d = u.shape
            sgn = jnp.where(jnp.arange(sl) % 2 == 0, 1.0, -1.0).astype(u.dtype)
            sgn3 = sgn[None, :, None]
            Vf = jnp.fft.rfft(phi, n=n, axis=0)
            Uf_p = jnp.fft.rfft(u, n=n, axis=1)
            Uf_m = jnp.fft.rfft(u * sgn3, n=n, axis=1)
            U_plus = jnp.fft.irfft(Vf[None, :, :, None] * Uf_p[:, :, None, :], n=n, axis=1)[:, :sl]
            U_minus = jnp.fft.irfft(Vf[None, :, :, None] * Uf_m[:, :, None, :], n=n, axis=1)[:, :sl]
            U_minus = U_minus * sgn[None, :, None, None]
            return (U_plus, U_minus)

        def _compute_spectral(u, sigma, phi, Mpp, Mpm):
            U_plus, U_minus = _stu_conv(phi, u, PADDED_SL)
            s = sigma ** SIGMA_POW
            out = jnp.einsum('btkd,k,kde->bte', U_plus, s, Mpp)
            out = out + jnp.einsum('btkd,k,kde->bte', U_minus, s, Mpm)
            return out

        def _compute_ar_u(Mu, u):
            sl = u.shape[1]
            out = jnp.zeros(u.shape[:2] + (Mu.shape[-1],), dtype=u.dtype)
            for i in range(Mu.shape[0]):
                ui = jnp.pad(u, ((0, 0), (i, 0), (0, 0)))[:, :sl]
                out = out + jnp.einsum('btd,de->bte', ui, Mu[i])
            return out

        def _stu(u, sigma, phi, Mu, Mpp, Mpm):
            return _compute_spectral(u, sigma, phi, Mpp, Mpm) + _compute_ar_u(Mu, u)
        key = jax.random.key(seed)
        ks = jax.random.split(key, 8)
        b, sl, d, K, k_u = (2, 2048, 64, 16, 3)
        x = jax.random.normal(ks[0], (b, sl, d), dtype=jnp.float32)
        sigma = jax.random.uniform(ks[1], (K,), dtype=jnp.float32, minval=0.001, maxval=1.0)
        phi = jax.random.normal(ks[2], (sl, K), dtype=jnp.float32) / np.sqrt(sl)
        M_u = jax.random.normal(ks[3], (4, k_u, d, d), dtype=jnp.float32) * 0.02
        M_phi_plus = jax.random.normal(ks[4], (4, K, d, d), dtype=jnp.float32) * 0.02
        M_phi_minus = jax.random.normal(ks[5], (4, K, d, d), dtype=jnp.float32) * 0.02
        log_weights = jnp.ones((4,), dtype=jnp.float32)
        u01 = jax.random.uniform(ks[6], (4,), dtype=jnp.float32, minval=1e-06, maxval=1.0 - 1e-06)
        gumbel = -jnp.log(-jnp.log(u01))
        return {'x': x, 'sigma': sigma, 'phi': phi, 'M_u': M_u, 'M_phi_plus': M_phi_plus, 'M_phi_minus': M_phi_minus, 'log_weights': log_weights, 'gumbel': gumbel}
    _L2_ffn_all = _L2_ffn_setup()
    _L2_ffn_in = {k: v for k, v in _L2_ffn_all.items() if k in ('sigma', 'phi', 'M_u', 'M_phi_plus', 'M_phi_minus', 'log_weights', 'gumbel')}
    del _L2_ffn_all

    def _L3_attn_setup():
        import jax, jax.numpy as jnp
        import numpy as np
        NEG = -1000000000000.0
        key = jax.random.key(seed)
        k1, k2, k3, k4 = jax.random.split(key, 4)
        B, T, D, U = (4, 2048, 64, 64)
        query = jax.random.normal(k1, (B, T, D), dtype=jnp.float32)
        s = 1.0 / np.sqrt(D)
        Wq = jax.random.normal(k2, (D, U), dtype=jnp.float32) * s
        Wk = jax.random.normal(k3, (D, U), dtype=jnp.float32) * s
        Wv = jax.random.normal(k4, (D, U), dtype=jnp.float32) * s
        return {'query': query, 'Wq': Wq, 'Wk': Wk, 'Wv': Wv}
    _L3_attn_all = _L3_attn_setup()
    _L3_attn_in = {k: v for k, v in _L3_attn_all.items() if k in ('Wq', 'Wk', 'Wv')}
    del _L3_attn_all

    def _L3_ffn_setup():
        import jax, jax.numpy as jnp
        import numpy as np
        B, N, D, C, E, K = (8, 4096, 64, 64, 8, 2)
        key = jax.random.key(seed)
        k0, k1, k2 = jax.random.split(key, 3)
        x = jax.random.normal(k0, (B, N, D), dtype=jnp.float32)
        router_w = jax.random.normal(k1, (D, E), dtype=jnp.float32) * 0.05
        router_b = jnp.zeros((E,), dtype=jnp.float32)
        expert_w = jax.random.normal(k2, (E, D, C), dtype=jnp.float32) * (1.0 / np.sqrt(D))
        expert_b = jnp.zeros((E, C), dtype=jnp.float32)
        return {'x': x, 'router_w': router_w, 'router_b': router_b, 'expert_w': expert_w, 'expert_b': expert_b}
    _L3_ffn_all = _L3_ffn_setup()
    _L3_ffn_in = {k: v for k, v in _L3_ffn_all.items() if k in ('router_w', 'router_b', 'expert_w', 'expert_b')}
    del _L3_ffn_all
    return {'x': x, 'L0_conv_w_off': _L0_conv_in['w_off'], 'L0_conv_b_off': _L0_conv_in['b_off'], 'L0_conv_w_main': _L0_conv_in['w_main'], 'L0_conv_b_main': _L0_conv_in['b_main'], 'L1_conv_W_in': _L1_conv_in['W_in'], 'L1_conv_conv_w': _L1_conv_in['conv_w'], 'L1_conv_conv_b': _L1_conv_in['conv_b'], 'L1_conv_W_x': _L1_conv_in['W_x'], 'L1_conv_W_dt': _L1_conv_in['W_dt'], 'L1_conv_b_dt': _L1_conv_in['b_dt'], 'L1_conv_A_log': _L1_conv_in['A_log'], 'L1_conv_D': _L1_conv_in['D'], 'L1_conv_W_out': _L1_conv_in['W_out'], 'L1_conv_gn_gamma': _L1_conv_in['gn_gamma'], 'L1_conv_gn_beta': _L1_conv_in['gn_beta'], 'L2_attn_Wq': _L2_attn_in['Wq'], 'L2_attn_bq': _L2_attn_in['bq'], 'L2_attn_Wk': _L2_attn_in['Wk'], 'L2_attn_bk': _L2_attn_in['bk'], 'L2_attn_Wv': _L2_attn_in['Wv'], 'L2_attn_bv': _L2_attn_in['bv'], 'L2_ffn_sigma': _L2_ffn_in['sigma'], 'L2_ffn_phi': _L2_ffn_in['phi'], 'L2_ffn_M_u': _L2_ffn_in['M_u'], 'L2_ffn_M_phi_plus': _L2_ffn_in['M_phi_plus'], 'L2_ffn_M_phi_minus': _L2_ffn_in['M_phi_minus'], 'L2_ffn_log_weights': _L2_ffn_in['log_weights'], 'L2_ffn_gumbel': _L2_ffn_in['gumbel'], 'L3_attn_Wq': _L3_attn_in['Wq'], 'L3_attn_Wk': _L3_attn_in['Wk'], 'L3_attn_Wv': _L3_attn_in['Wv'], 'L3_ffn_router_w': _L3_ffn_in['router_w'], 'L3_ffn_router_b': _L3_ffn_in['router_b'], 'L3_ffn_expert_w': _L3_ffn_in['expert_w'], 'L3_ffn_expert_b': _L3_ffn_in['expert_b']}

def reference(x, L0_conv_w_off, L0_conv_b_off, L0_conv_w_main, L0_conv_b_main, L1_conv_W_in, L1_conv_conv_w, L1_conv_conv_b, L1_conv_W_x, L1_conv_W_dt, L1_conv_b_dt, L1_conv_A_log, L1_conv_D, L1_conv_W_out, L1_conv_gn_gamma, L1_conv_gn_beta, L2_attn_Wq, L2_attn_bq, L2_attn_Wk, L2_attn_bk, L2_attn_Wv, L2_attn_bv, L2_ffn_sigma, L2_ffn_phi, L2_ffn_M_u, L2_ffn_M_phi_plus, L2_ffn_M_phi_minus, L2_ffn_log_weights, L2_ffn_gumbel, L3_attn_Wq, L3_attn_Wk, L3_attn_Wv, L3_ffn_router_w, L3_ffn_router_b, L3_ffn_expert_w, L3_ffn_expert_b):
    import jax
    import jax.numpy as jnp

    def _L0_conv_ref(x, w_off, b_off, w_main, b_main):
        import jax, jax.numpy as jnp
        import numpy as np
        K = 3
        STRIDE = 1
        PADDING = 1

        def _conv2d(x, w, b, stride, padding):
            out = jax.lax.conv_general_dilated(x, w, window_strides=(stride, stride), padding=[(padding, padding), (padding, padding)], dimension_numbers=('NCHW', 'OIHW', 'NCHW'))
            return out + b[None, :, None, None]

        def _grid_sample_bilinear_zeros(x, grid):
            B, C, Hin, Win = x.shape
            gx = (grid[..., 0] + 1.0) * (Win * 0.5) - 0.5
            gy = (grid[..., 1] + 1.0) * (Hin * 0.5) - 0.5
            x0f = jnp.floor(gx)
            y0f = jnp.floor(gy)
            wx1 = gx - x0f
            wy1 = gy - y0f
            x0 = x0f.astype(jnp.int32)
            y0 = y0f.astype(jnp.int32)
            xf = x.reshape(B, C, Hin * Win)

            def gather(yi, xi):
                valid = (xi >= 0) & (xi < Win) & (yi >= 0) & (yi < Hin)
                idx = jnp.clip(yi, 0, Hin - 1) * Win + jnp.clip(xi, 0, Win - 1)
                g = jax.vmap(lambda xb, ib: xb[:, ib])(xf, idx)
                return g * valid[:, None, :, :].astype(x.dtype)
            w00 = ((1.0 - wx1) * (1.0 - wy1))[:, None]
            w01 = (wx1 * (1.0 - wy1))[:, None]
            w10 = ((1.0 - wx1) * wy1)[:, None]
            w11 = (wx1 * wy1)[:, None]
            return gather(y0, x0) * w00 + gather(y0, x0 + 1) * w01 + gather(y0 + 1, x0) * w10 + gather(y0 + 1, x0 + 1) * w11
        offset = _conv2d(x, w_off, b_off, STRIDE, PADDING)
        B, _, H, W = offset.shape
        off = jnp.transpose(offset, (0, 2, 3, 1)).reshape(B, H, W, K, K, 2)
        ox = jnp.cumsum(off[:, :, :, :, 0, 0], axis=3)
        oy = jnp.cumsum(off[:, :, :, 0, :, 1], axis=3)
        ox_f = jnp.broadcast_to(ox[..., None], (B, H, W, K, K))
        oy_f = jnp.broadcast_to(oy[:, :, :, None, :], (B, H, W, K, K))
        off_f = jnp.stack([ox_f, oy_f], axis=-1).reshape(B, H, W, K * K, 2)
        y_range = jnp.linspace(-1.0, 1.0, H, dtype=x.dtype)
        x_range = jnp.linspace(-1.0, 1.0, W, dtype=x.dtype)
        yg, xg = jnp.meshgrid(y_range, x_range, indexing='ij')
        base = jnp.stack((xg, yg), axis=-1)
        grid = base[None, :, :, None, :] + off_f
        grid = grid.reshape(B, H, W * K * K, 2)
        xs = _grid_sample_bilinear_zeros(x, grid)
        C = x.shape[1]
        xs = xs.reshape(B, C, H, W, K * K)
        wm = w_main.reshape(w_main.shape[0], C, K * K)
        out = jnp.einsum('bchwk,ock->bohw', xs, wm)
        return out + b_main[None, :, None, None]

    def _L1_conv_ref(x_hsi, W_in, conv_w, conv_b, W_x, W_dt, b_dt, A_log, D, W_out, gn_gamma, gn_beta):
        import jax, jax.numpy as jnp
        import numpy as np
        D_MODEL = 64
        D_STATE = 16
        D_CONV = 2
        EXPAND = 2
        D_INNER = EXPAND * D_MODEL
        DT_RANK = (D_MODEL + 15) // 16
        GROUPS = 4
        EPS = 1e-05

        def _causal_conv_k2(x, w, b):
            xp = jnp.pad(x, ((0, 0), (1, 0), (0, 0)))
            return xp[:, :-1] * w[:, 0] + xp[:, 1:] * w[:, 1] + b

        def _selective_scan(xc, dt, Bmat, Cmat, A, D):

            def step(h, inp):
                dt_t, B_t, C_t, x_t = inp
                dA = jnp.exp(dt_t[..., None] * A)
                dBx = dt_t[..., None] * B_t[:, None, :] * x_t[..., None]
                h = dA * h + dBx
                y = jnp.einsum('bdn,bn->bd', h, C_t)
                return (h, y)
            B_, L, Din = xc.shape
            h0 = jnp.zeros((B_, Din, A.shape[1]), dtype=xc.dtype)
            xs = (jnp.swapaxes(dt, 0, 1), jnp.swapaxes(Bmat, 0, 1), jnp.swapaxes(Cmat, 0, 1), jnp.swapaxes(xc, 0, 1))
            _, ys = jax.lax.scan(step, h0, xs)
            return jnp.swapaxes(ys, 0, 1) + xc * D

        def _mamba(x, W_in, conv_w, conv_b, W_x, W_dt, b_dt, A_log, D, W_out):
            xz = x @ W_in
            xh, z = jnp.split(xz, 2, axis=-1)
            xh = jax.nn.silu(_causal_conv_k2(xh, conv_w, conv_b))
            x_dbl = xh @ W_x
            dt_low = x_dbl[..., :DT_RANK]
            Bmat = x_dbl[..., DT_RANK:DT_RANK + D_STATE]
            Cmat = x_dbl[..., DT_RANK + D_STATE:]
            dt = jax.nn.softplus(dt_low @ W_dt + b_dt)
            A = -jnp.exp(A_log)
            y = _selective_scan(xh, dt, Bmat, Cmat, A, D)
            y = y * jax.nn.silu(z)
            return y @ W_out

        def _group_norm(x, gamma, beta):
            B_, C, H, W = x.shape
            xr = x.reshape(B_, GROUPS, -1)
            mean = xr.mean(-1, keepdims=True)
            var = xr.var(-1, keepdims=True)
            xn = ((xr - mean) * jax.lax.rsqrt(var + EPS)).reshape(B_, C, H, W)
            return xn * gamma[:, None, None] + beta[:, None, None]
        B_, C, H, W = x_hsi.shape
        x = jnp.transpose(x_hsi, (0, 2, 3, 1)).reshape(B_, H * W, C)
        x = _mamba(x, W_in, conv_w, conv_b, W_x, W_dt, b_dt, A_log, D, W_out)
        x = jnp.transpose(x.reshape(B_, H, W, C), (0, 3, 1, 2))
        x = jax.nn.silu(_group_norm(x, gn_gamma, gn_beta))
        return x + x_hsi

    def _L2_attn_ref(inputs, Wq, bq, Wk, bk, Wv, bv):
        import jax, jax.numpy as jnp
        import numpy as np
        B, N, D = (4, 512, 64)
        q = inputs @ Wq + bq
        k = inputs @ Wk + bk
        v = inputs @ Wv + bv
        kv = jnp.sum(k * v, axis=1, keepdims=True)
        return q * kv

    def _L2_ffn_ref(x, sigma, phi, M_u, M_phi_plus, M_phi_minus, log_weights, gumbel):
        import jax, jax.numpy as jnp
        import numpy as np
        PADDED_SL = 4096
        TEMPERATURE = 1.0
        SIGMA_POW = 0.25

        def _stu_conv(phi, u, n):
            b, sl, d = u.shape
            sgn = jnp.where(jnp.arange(sl) % 2 == 0, 1.0, -1.0).astype(u.dtype)
            sgn3 = sgn[None, :, None]
            Vf = jnp.fft.rfft(phi, n=n, axis=0)
            Uf_p = jnp.fft.rfft(u, n=n, axis=1)
            Uf_m = jnp.fft.rfft(u * sgn3, n=n, axis=1)
            U_plus = jnp.fft.irfft(Vf[None, :, :, None] * Uf_p[:, :, None, :], n=n, axis=1)[:, :sl]
            U_minus = jnp.fft.irfft(Vf[None, :, :, None] * Uf_m[:, :, None, :], n=n, axis=1)[:, :sl]
            U_minus = U_minus * sgn[None, :, None, None]
            return (U_plus, U_minus)

        def _compute_spectral(u, sigma, phi, Mpp, Mpm):
            U_plus, U_minus = _stu_conv(phi, u, PADDED_SL)
            s = sigma ** SIGMA_POW
            out = jnp.einsum('btkd,k,kde->bte', U_plus, s, Mpp)
            out = out + jnp.einsum('btkd,k,kde->bte', U_minus, s, Mpm)
            return out

        def _compute_ar_u(Mu, u):
            sl = u.shape[1]
            out = jnp.zeros(u.shape[:2] + (Mu.shape[-1],), dtype=u.dtype)
            for i in range(Mu.shape[0]):
                ui = jnp.pad(u, ((0, 0), (i, 0), (0, 0)))[:, :sl]
                out = out + jnp.einsum('btd,de->bte', ui, Mu[i])
            return out

        def _stu(u, sigma, phi, Mu, Mpp, Mpm):
            return _compute_spectral(u, sigma, phi, Mpp, Mpm) + _compute_ar_u(Mu, u)
        T = x.shape[1]
        outs = []
        for i, frac in enumerate((1, 2, 4, 8)):
            xi = x[:, :T // frac]
            si = _stu(xi, sigma, phi, M_u[i], M_phi_plus[i], M_phi_minus[i])
            si = jnp.pad(si, ((0, 0), (0, T - si.shape[1]), (0, 0)))
            outs.append(si)
        y_soft = jax.nn.softmax((log_weights + gumbel) / TEMPERATURE)
        y_hard = jax.nn.one_hot(jnp.argmax(y_soft), 4, dtype=y_soft.dtype)
        weights = y_hard - jax.lax.stop_gradient(y_soft) + y_soft
        stacked = jnp.stack(outs, axis=-1)
        return jnp.sum(stacked * weights, axis=-1)

    def _L3_attn_ref(query, Wq, Wk, Wv):
        import jax, jax.numpy as jnp
        import numpy as np
        NEG = -1000000000000.0
        q = jnp.einsum('btd,du->btu', query, Wq)
        k = jnp.einsum('btd,du->btu', query, Wk)
        v = jnp.einsum('btd,du->btu', query, Wv)
        T = v.shape[1]
        scores = jnp.einsum('bqu,bku->bqk', q, k) / jnp.sqrt(jnp.asarray(T, jnp.float32))
        causal = jnp.tril(jnp.ones((T, T), dtype=jnp.float32))
        scores = scores + NEG * (1.0 - causal)
        attn = jax.nn.softmax(scores, axis=-1)
        context = jnp.einsum('bqk,bku->bqu', attn, v)
        return context

    def _L3_ffn_ref(x, router_w, router_b, expert_w, expert_b):
        import jax, jax.numpy as jnp
        import numpy as np
        B, N, D, C, E, K = (8, 4096, 64, 64, 8, 2)
        router_probs = jax.nn.softmax(x @ router_w + router_b, axis=-1)
        top_p, top_i = jax.lax.top_k(router_probs, K)
        top_p = top_p / jnp.sum(top_p, axis=-1, keepdims=True)
        expert_out = jnp.einsum('bnd,edc->bnec', x, expert_w) + expert_b
        gathered = jnp.take_along_axis(expert_out, top_i[..., None], axis=2)
        return jnp.einsum('bnk,bnkc->bnc', top_p, gathered)

    def _gn(v, G=32, eps=1e-05):
        B_, C_, H_, W_ = v.shape
        g = v.reshape(B_, G, C_ // G, H_, W_)
        m = jnp.mean(g, axis=(2, 3, 4), keepdims=True)
        s = jnp.var(g, axis=(2, 3, 4), keepdims=True)
        return ((g - m) / jnp.sqrt(s + eps)).reshape(v.shape)

    def _ln_c(v, eps=1e-06):
        m = jnp.mean(v, axis=1, keepdims=True)
        s = jnp.var(v, axis=1, keepdims=True)
        return (v - m) / jnp.sqrt(s + eps)

    def _ln_t(v, eps=1e-05):
        m = jnp.mean(v, axis=-1, keepdims=True)
        s = jnp.var(v, axis=-1, keepdims=True)
        return (v - m) / jnp.sqrt(s + eps)

    def _to_tokens(v):
        B_, C_, H_, W_ = v.shape
        return v.reshape(B_, C_, H_ * W_).transpose(0, 2, 1)

    def _from_tokens(t, like):
        B_, C_, H_, W_ = like.shape
        return t.transpose(0, 2, 1).reshape(B_, C_, H_, W_)
    x = x + _L0_conv_ref(_gn(x), L0_conv_w_off, L0_conv_b_off, L0_conv_w_main, L0_conv_b_main)
    x = _L1_conv_ref(x, L1_conv_W_in, L1_conv_conv_w, L1_conv_conv_b, L1_conv_W_x, L1_conv_W_dt, L1_conv_b_dt, L1_conv_A_log, L1_conv_D, L1_conv_W_out, L1_conv_gn_gamma, L1_conv_gn_beta)
    t = _to_tokens(x)
    t = t + _L2_attn_ref(_ln_t(t), L2_attn_Wq, L2_attn_bq, L2_attn_Wk, L2_attn_bk, L2_attn_Wv, L2_attn_bv)
    t = t + _L2_ffn_ref(_ln_t(t), L2_ffn_sigma, L2_ffn_phi, L2_ffn_M_u, L2_ffn_M_phi_plus, L2_ffn_M_phi_minus, L2_ffn_log_weights, L2_ffn_gumbel)
    t = t + _L3_attn_ref(_ln_t(t), L3_attn_Wq, L3_attn_Wk, L3_attn_Wv)
    t = t + _L3_ffn_ref(_ln_t(t), L3_ffn_router_w, L3_ffn_router_b, L3_ffn_expert_w, L3_ffn_expert_b)
    x = _from_tokens(t, x)
    return x

_drawn_inputs = setup_inputs


def setup_inputs(seed=0):
    import zlib

    import numpy as np

    out = dict(_drawn_inputs(seed))
    spreads = {'L0_conv_b_off': (0.0, 0.1),
     'L0_conv_b_main': (0.0, 0.1),
     'L1_conv_D': (1.0, 0.2),
     'L1_conv_gn_gamma': (1.0, 0.2),
     'L1_conv_gn_beta': (0.0, 0.1),
     'L2_attn_bq': (0.0, 0.1),
     'L2_attn_bk': (0.0, 0.1),
     'L2_attn_bv': (0.0, 0.1),
     'L2_ffn_log_weights': (1.0, 0.2),
     'L3_ffn_router_b': (0.0, 2.0),
     'L3_ffn_expert_b': (0.0, 2.0)}
    factors = {'L1_conv_W_x': 8.0,
     'L1_conv_W_dt': 64.0,
     'L1_conv_b_dt': 33.648,
     'L1_conv_A_log': 64.0,
     'L2_ffn_sigma': 8.0,
     'L2_ffn_phi': 8.0,
     'L2_ffn_M_u': 28.164,
     'L2_ffn_M_phi_plus': 8.0,
     'L2_ffn_M_phi_minus': 8.0,
     'L2_ffn_gumbel': 8.0,
     'L3_attn_Wq': 8.0,
     'L3_attn_Wk': 8.0,
     'L3_attn_Wv': 8.0,
     'L3_ffn_router_w': 8.0,
     'L3_ffn_expert_w': 8.0}
    for name, (base, spread) in spreads.items():
        noise = np.random.default_rng([zlib.crc32(name.encode()), seed]).standard_normal(out[name].shape)
        drawn = base * np.exp(spread * noise) if base else spread * noise
        out[name] = jnp.asarray(drawn.astype(out[name].dtype))
    for name, factor in factors.items():
        out[name] = (out[name] * factor).astype(out[name].dtype)
    return out
```

```python
from contextlib import ExitStack

import numpy as np

import concourse.bass as bass
from concourse import mybir

F32 = mybir.dt.float32
BF16 = mybir.dt.bfloat16
I32 = mybir.dt.int32
U32 = mybir.dt.uint32
ALU = mybir.AluOpType
ACT = mybir.ActivationFunctionType
AX = mybir.AxisListType

P = 128
BATCH, C, H, W = 8, 64, 32, 32
L = H * W
PAIRS = BATCH // 2
BLK = L // P
TAPS = 9
KTILES = (TAPS + 1) // 2
SIDE = H + 4
CORNERS = 4
N_STATE = 16
DT_RANK = 4
FILTERS = 16
EXPERTS = 8
STU_EXPERTS = 4
HALF = L // 2
TOEP = HALF + 1
GROUPS = 2 * BLK
SLOTS = 2
NEG = -1.0e12
SCORE_SCALE = 1.0 / float(np.sqrt(L))
SEGMENTS = [(0, 64, 0), (64, 128, 1), (128, 256, 2), (256, 512, 3)]

DVE_STEPS = 139
ACT_STEPS = 6


class Signal:

    def __init__(self, sem, per_pair, base):
        self.sem, self.per_pair, self.base, self.raised = sem, per_pair, base, 0

    def up(self, n=1):
        self.raised += n
        return self.sem, n

    def at(self, i, n):
        return self.sem, i * self.per_pair + (n + self.base)


def shape_constants():
    r = np.arange(P)
    ident = np.eye(P)
    mean_of = lambda g: (r[:, None] // g == r[None, :] // g) / g
    mask = np.where(r[None, :] > r[:, None], NEG / SCORE_SCALE, 0.0)
    tok = np.arange(L).reshape(BLK, P)
    lin = np.linspace(-1.0, 1.0, H).astype(np.float32)
    base = np.zeros((P, 2, BLK, 2, 3))
    base[:, :, :, 0, :] = lin[tok % W].T[:, None, :, None]
    base[:, :, :, 1, :] = lin[tok // W].T[:, None, :, None]
    rank = np.broadcast_to(np.arange(EXPERTS, 0, -1), (P, EXPERTS))
    pick = (r[:, None] % 32 == np.arange(32)[None, :]) * 1.0
    parts = [ident, mean_of(2), mean_of(16), mean_of(64), mask, base.reshape(P, -1), rank, pick]
    return np.ascontiguousarray(np.concatenate(parts, 1).astype(np.float32))


def hybrid_kernel(nc, x, consts, w_off, b_off, w_main, b_main, W_in, conv_w, conv_b, W_x, W_dt, b_dt,
                  A_log, D, W_out, gn_gamma, gn_beta, Wq2, bq2, Wk2, bk2, Wv2, bv2, sigma, phi_pad,
                  M_u, M_plus, M_minus, log_weights, gumbel, Wq3, Wk3, Wv3, router_w, router_b,
                  expert_w, expert_b, tables, out, dbg=None):
    ctx = ExitStack()
    with ctx:
        def sb(name, shape, dt=F32):
            return ctx.enter_context(nc.sbuf_tensor(name, shape, dt))

        def sig(name, per_pair=0, base=0):
            s = Signal(ctx.enter_context(nc.semaphore(name)), per_pair, base)
            signals.append((name, s))
            return s

        signals = []
        v, a, g, t = nc.vector, nc.scalar, nc.gpsimd, nc.tensor

        cst = sb("cst", [P, consts.shape[1]])
        ident, mean2, mean16, mean64, mask = (cst[:, P * n:P * n + P] for n in range(5))
        base = cst[:, 5 * P:5 * P + 96].rearrange("p (g a k) -> p g a k", g=GROUPS, a=2)
        rank = cst[:, 5 * P + 96:5 * P + 104]
        pick = cst[:, 5 * P + 104:5 * P + 136]
        woff = sb("woff", [P, TAPS, 2, 18])
        wmain = sb("wmain", [P, KTILES, 2, P])
        win = sb("win", [P, 2, 4 * C])
        wxdt = sb("wxdt", [P, DT_RANK])
        wxbc = sb("wxbc", [P, 96])
        wdt = sb("wdt", [DT_RANK, P])
        wout = sb("wout", [P, 2, P])
        sel = sb("sel", [96, 32, P], BF16)
        negA = sb("negA", [P, N_STATE])
        wqkv2 = sb("wqkv2", [P, 3, P])
        wqkv3 = sb("wqkv3", [P, 3, P])
        wrouter = sb("wrouter", [P, 2, EXPERTS])
        wexp = sb("wexp", [P, EXPERTS, C])
        bexp = sb("bexp", [2 * EXPERTS, P])
        boff = sb("boff", [P, 18])
        brouter = sb("brouter", [P, EXPERTS])
        cols = sb("cols", [P, 12])
        (bmain, cw0, cw1, cb, bdt, dskip, gamma, beta, bq, bk, bv, eps) = (cols[:, n:n + 1] for n in range(12))
        mspec = sb("mspec", [P, 4, 2, FILTERS, C])
        mar = sb("mar", [P, 4, 3, C])
        mixw = sb("mixw", [P, 40])
        spow = sb("spow", [P, FILTERS])

        xin = sb("xin", [P, L])
        X = sb("X", [P, L])
        xpad = sb("xpad", [P, 3, H + 2, W])
        slots = [sb(f"slot{n}", [P, TAPS, CORNERS, C]) for n in range(SLOTS)]
        samples = [sb(f"samples{n}", [P, TAPS, C]) for n in range(2)]
        coord = sb("coord", [P, 7, 96])
        wsplit = sb("wsplit", [P, GROUPS, 2, 3, 2])
        index = sb("index", [P, GROUPS, TAPS], U32)
        cweight = sb("cweight", [P, GROUPS, CORNERS, TAPS])
        small = sb("small", [P, 64])
        F = sb("F", [P, 18, L])
        toep = [sb(f"toep{n}", [P, 2, TOEP]) for n in range(2)]
        upad = sb("upad", [P, 2 + L])
        route = sb("route", [P, 12, GROUPS, EXPERTS])
        rtop = sb("rtop", [P, 6, GROUPS])

        def f(n):
            return F[:, n, :]

        ps = [ctx.enter_context(nc.psum_tensor(f"ps{n}", [P, L], F32)) for n in range(4)]

        zeroed = sig("zeroed")
        loaded = sig("loaded")
        tabled = sig("tabled")
        mraw_in = sig("mraw_in")
        boot_v = sig("boot_v")
        boot_a = sig("boot_a")
        ready = sig("ready")
        boot_s = sig("boot_s")
        vstep = sig("vstep", DVE_STEPS)
        astep = sig("astep", ACT_STEPS)
        xin_in = sig("xin_in", 16)
        stat_in = sig("stat_in", 2)
        stat_out = sig("stat_out", 2)
        var_ok = sig("var_ok", 2)
        rstd_ok = sig("rstd_ok", 2)
        xn_ok = sig("xn_ok", 1)
        xnT_ps = sig("xnT_ps", 1)
        xnT_ok = sig("xnT_ok", 1)
        off_ps = sig("off_ps", 1)
        off_read = sig("off_read", 1)
        table_in = sig("table_in", 16 * 32)
        pool_tick = sig("pool_tick", GROUPS, base=1)
        index_ok = sig("index_ok", 1)
        weight_ok = sig("weight_ok", 1)
        gathered = [sig(f"gathered{n}", 16 * TAPS * GROUPS // SLOTS) for n in range(SLOTS)]
        sample_ok = sig("sample_ok", GROUPS, base=1)
        sample_ps = sig("sample_ps", GROUPS)
        sampleT = sig("sampleT", GROUPS)
        conv_q = sig("conv_q", 4)
        x1_ok = sig("x1_ok", 1, base=1)
        xz_ps = sig("xz_ps", 4)
        xh_pre = sig("xh_pre", 2)
        conv2 = sig("conv2", 2)
        xc_ok = sig("xc_ok", 2)
        xdbl_ps = sig("xdbl_ps", 4)
        bc_hi = sig("bc_hi", 2)
        bc_ok = sig("bc_ok", 2)
        dtlow_ok = sig("dtlow_ok", 2)
        dtp_ps = sig("dtp_ps", 2)
        sp_in = sig("sp_in", 2)
        dtp_read = sig("dtp_read", 2)
        sp_exp = sig("sp_exp", 2)
        sp_ln = sig("sp_ln", 2)
        dt_ok = sig("dt_ok", 2)
        dA_ok = sig("dA_ok", 2 * N_STATE)
        scan_ok = sig("scan_ok", 2 * N_STATE)
        bcast = sig("bcast", 4 * N_STATE)
        bin_ok = sig("bin_ok", 2 * N_STATE)
        hc_ok = sig("hc_ok", 2 * N_STATE)
        ysum = sig("ysum", 2 * N_STATE)
        y2_ok = sig("y2_ok", 2)
        mout_ps = sig("mout_ps", 1)
        aff_ok = sig("aff_ok", 1)
        gns_ok = sig("gns_ok", 1)
        ln_x = sig("ln_x", 4)
        ln_mean = sig("ln_mean", 4)
        ln_cent = sig("ln_cent", 4)
        ln_sq = sig("ln_sq", 4)
        ln_var = sig("ln_var", 4)
        ln_rstd = sig("ln_rstd", 4)
        ln_ok = sig("ln_ok", 4)
        lin_ps = sig("lin_ps", 3)
        lk_ok = sig("lk_ok", 1)
        lin_done = sig("lin_done", 1)
        urev_ok = sig("urev_ok", 1)
        uT_ps = sig("uT_ps", 1)
        uT_ok = sig("uT_ok", 1)
        toep_in = [sig(f"toep_in{n}", 16 * FILTERS // 2) for n in range(2)]
        conv_ps = sig("conv_ps", 4 * FILTERS, base=1)
        conv_a = sig("conv_a", 2 * FILTERS)
        conv_v = sig("conv_v", 2 * FILTERS)
        conv_used = sig("conv_used", 4 * FILTERS)
        stu_ps = sig("stu_ps", 1)
        stu_done = sig("stu_done", 1)
        qkv_ps = sig("qkv_ps", 3)
        qkv_ok = sig("qkv_ok", 3)
        score_ps = sig("score_ps", GROUPS)
        negmax = sig("negmax", GROUPS)
        probs = sig("probs", GROUPS)
        pT_ps = sig("pT_ps", GROUPS)
        pT_ok = sig("pT_ok", GROUPS)
        ctx_ps = sig("ctx_ps", GROUPS)
        ctx_ok = sig("ctx_ok", GROUPS)
        ctxT_ps = sig("ctxT_ps", 1)
        att_done = sig("att_done", 1)
        log_ps = sig("log_ps", 1)
        top_in = sig("top_in", 1)
        top_exp = sig("top_exp", 1)
        gate_ok = sig("gate_ok", 1)
        gateT_ps = sig("gateT_ps", 1)
        gateT_ok = sig("gateT_ok", 1)
        exp_ps = sig("exp_ps", GROUPS)
        exp_read = sig("exp_read", GROUPS)
        moe_ok = sig("moe_ok", GROUPS)
        moe_ps = sig("moe_ps", 1)
        out_ok = sig("out_ok", 1, base=1)
        stored = sig("stored", 16, base=1)
        dbg_in = sig("dbg_in", 16 * 5)

        x_v = x.rearrange("(i b) c h w -> i (b c) (h w)", b=2)
        out_v = out.rearrange("(i b) c h w -> i (b c) (h w)", b=2)
        col_of = lambda w: w.rearrange("(p a) -> p a", a=1)
        row_of = lambda w: w.rearrange("(a p) -> a p", a=1)
        bcast_row = lambda w: row_of(w).broadcast_to([P, w.shape[0]])

        block = ctx.enter_context(nc.Block())

        @block.sync
        def _(sp):
            def load(dst, src, s=loaded):
                sp.dma_start(dst, src).then_inc(*s.up(16))

            load(cst[:], consts)
            for h in range(2):
                r = slice(C * h, C * h + C)
                load(F[r, 0:4, :].rearrange("p n l -> p (n l)").rearrange("p (i k e) -> p i k e", i=4, e=C), M_plus.rearrange("i k d e -> d i k e"), mraw_in)
                load(F[r, 4:8, :].rearrange("p n l -> p (n l)").rearrange("p (i k e) -> p i k e", i=4, e=C), M_minus.rearrange("i k d e -> d i k e"), mraw_in)
                load(F[r, 8, 0:12 * C].rearrange("p (i r e) -> p i r e", i=4, e=C), M_u.rearrange("i r d e -> d i r e"), mraw_in)
            load(mixw[:, 0:4], bcast_row(log_weights), mraw_in)
            load(mixw[:, 4:8], bcast_row(gumbel), mraw_in)
            load(spow[:], bcast_row(sigma), mraw_in)
            sp.wait_ge(*zeroed.at(0, 1))
            for h in range(2):
                r = slice(C * h, C * h + C)
                load(woff[r, :, h, :], w_off)
                for kk in range(KTILES):
                    for aa in range(2 if kk < KTILES - 1 else 1):
                        load(wmain[C * aa:C * aa + C, kk, h, r], w_main[2 * kk + aa])
                load(win[r, h, :], W_in)
                load(wout[:, h, r], W_out)
                for n, w in enumerate((Wq2, Wk2, Wv2)):
                    load(wqkv2[r, n, r], w)
                for n, w in enumerate((Wq3, Wk3, Wv3)):
                    load(wqkv3[r, n, r], w)
                load(wrouter[r, h, :], router_w)
                load(wexp[r, :, :], expert_w.rearrange("e d c -> d e c"))
                load(bexp[EXPERTS * h:EXPERTS * h + EXPERTS, r], expert_b)
                for dst, src in ((bmain, b_main), (gamma, gn_gamma), (beta, gn_beta), (bq, bq2), (bk, bk2), (bv, bv2)):
                    load(dst[r, :], col_of(src))
            for dst, src in ((cb, conv_b), (bdt, b_dt), (dskip, D)):
                load(dst, col_of(src))
            load(cols[:, 1:3], conv_w)
            load(wxdt[:], W_x[:, 0:DT_RANK])
            for q in range(3):
                load(wxbc[:, 32 * q:32 * q + 32], W_x[:, DT_RANK:])
            load(wdt[:], W_dt)
            load(negA[:], A_log)
            load(boff[:], bcast_row(b_off))
            load(brouter[:], bcast_row(router_b))
            sp.wait_ge(*boot_s.at(0, 1))
            for tb in tables:
                tv = tb.rearrange("r c -> (r c)").rearrange("(p q) -> p q", p=P)
                half = tv.shape[1] // 2
                for hh in range(2):
                    load(tv[:, half * hh:half * hh + half], F[:, 9:11, :].rearrange("p n l -> p (n l)")[:, 0:half], tabled)

            with sp.Fori(0, PAIRS) as i:
                def dstore(n):
                    if dbg:
                        sp.wait_ge(*(x1_ok.at(i, 1) if n == 0 else ln_x.at(i, n)))
                        sp.dma_start(dbg[n].rearrange("(i b) c h w -> i (b c) (h w)", b=2)[i], X[:]).then_inc(*dbg_in.up(16))
                sp.wait_ge(*x1_ok.at(i, 0))
                sp.dma_start(xin[:], x_v[i]).then_inc(*xin_in.up(16))
                sp.wait_ge(*xnT_ok.at(i, 1))
                sp.wait_ge(*tabled.at(0, 64))
                xnT = f(0).rearrange("p (n c) -> p n c", n=BLK)
                for h in range(2):
                    tb = tables[h].rearrange("(y x) (k c) -> y x k c", x=SIDE, c=C)
                    for k in range(CORNERS):
                        dy, dx = k // 2, k % 2
                        for yy in range(4):
                            dst = tb[2 - dy + yy:2 - dy + yy + 4 * (BLK - 1) + 1:4, 2 - dx:2 - dx + W, k, :]
                            sp.dma_start(dst.rearrange("n x c -> x n c"),
                                         xnT[32 * yy:32 * yy + 32, :, C * h:C * h + C]).then_inc(*table_in.up(16))
                dstore(0), dstore(1), dstore(2)
                for k in range(FILTERS):
                    sp.wait_ge(*conv_ps.at(i, max(4 * (k - 1), 0)))
                    src = bass.AP(phi_pad.tensor, k * 2 * (P + HALF), [[1, P], [P + HALF, 2], [1, TOEP]])
                    sp.dma_start(toep[k % 2][:], src).then_inc(*toep_in[k % 2].up(16))
                dstore(3), dstore(4)
                sp.wait_ge(*out_ok.at(i, 1))
                sp.dma_start(out_v[i], f(17)).then_inc(*stored.up(16))
            sp.wait_ge(stored.sem, 16 * PAIRS + stored.base)
                
        @block.gpsimd
        def _(pool):
            pool.wait_ge(*ready.at(0, 1))
            with pool.Fori(0, PAIRS) as i:
                pool.wait_ge(*index_ok.at(i, 1))
                pool.wait_ge(*table_in.at(i, 16 * 32))
                for m in range(GROUPS):
                    pool.wait_ge(*pool_tick.at(i, m))
                    pool.wait_ge(*sample_ok.at(i, 0 if m < SLOTS else m - SLOTS + 1))
                    g.tensor_tensor(small[:, 42:43], eps, eps, ALU.add).then_inc(*pool_tick.up())
                    slot = slots[m % SLOTS]
                    for k in range(TAPS):
                        g.indirect_dma_start(
                            out=slot[:, k, :, :].rearrange("p a c -> p (a c)"), out_offset=None, in_=tables[m // BLK],
                            in_offset=bass.IndirectOffsetOnAxis(ap=index[:, m, k:k + 1], axis=0),
                        ).then_inc(*gathered[m % SLOTS].up(16))

        @block.scalar
        def _(act):
            def link(ins, i):
                ins.then_inc(*astep.up())
                act.wait_ge(*astep.at(i, astep.raised))

            def rstd(out_ap, in_ap, i, bias=0.0):
                link(a.activation(out_ap, in_ap, ACT.Ln, bias=bias), i)
                return a.activation(out_ap, out_ap, ACT.Exp, scale=-0.5)

            act.wait_ge(*mraw_in.at(0, 16 * 9))
            a.activation(spow[:], spow[:], ACT.Ln).then_inc(*boot_a.up())
            act.wait_ge(*boot_a.at(0, 1))
            a.activation(spow[:], spow[:], ACT.Exp, scale=0.25).then_inc(*boot_a.up())
            act.wait_ge(*boot_v.at(0, 3))
            a.activation(mixw[:, 12:16], mixw[:, 8:12], ACT.Exp).then_inc(*boot_a.up())
            act.wait_ge(*loaded.at(0, loaded.raised))
            act.wait_ge(*boot_v.at(0, 4))
            a.activation(negA[:], negA[:], ACT.Exp).then_inc(*boot_a.up())
            act.wait_ge(*ready.at(0, 1))

            def layer_norm(n, i):
                act.wait_ge(*ln_cent.at(i, n + 1))
                a.activation(f(13), f(12), ACT.Square).then_inc(*ln_sq.up())
                act.wait_ge(*ln_var.at(i, n + 1))
                link(a.activation(f(13), ps[1][:], ACT.Ln, bias=eps), i)
                a.activation(f(13), f(13), ACT.Exp, scale=-0.5).then_inc(*ln_rstd.up())

            with act.Fori(0, PAIRS) as i:
                astep.raised = 0
                act.wait_ge(*var_ok.at(i, 1))
                rstd(small[:, 20:21], small[:, 19:20], i).then_inc(*rstd_ok.up())
                act.wait_ge(*xnT_ps.at(i, 1))
                a.copy(f(0), ps[0][:]).then_inc(*xnT_ok.up())
                for m in range(GROUPS):
                    q, col = m // 4, P * (m % 4)
                    act.wait_ge(*sample_ps.at(i, m + 1))
                    if q >= 2:
                        act.wait_ge(*conv_q.at(i, q - 1))
                    st = F[:, 2 + 3 * (q % 2):5 + 3 * (q % 2), :].rearrange("p n l -> p (n l)")[:, 0:KTILES * HALF].rearrange("p (k q) -> p k q", k=KTILES)
                    src = ps[2 + m % 2][:].rearrange("p (k q) -> p k q", q=P)
                    a.copy(st[:, 0:4, col:col + P], src[:, 0:4, :])
                    a.copy(st[0:C, 4, col:col + P], src[0:C, 4, :]).then_inc(*sampleT.up())
                for h in range(2):
                    act.wait_ge(*xz_ps.at(i, 2 * h + 1))
                    a.activation(f(0), ps[0][:], ACT.Identity, bias=cb, scale=cw1).then_inc(*xh_pre.up())
                    if h == 1:
                        act.wait_ge(*y2_ok.at(i, 1))
                    act.wait_ge(*xz_ps.at(i, 2 * h + 2))
                    a.activation(f(1), ps[1][:], ACT.Silu)
                    act.wait_ge(*conv2.at(i, h + 1))
                    a.activation(f(2), f(0), ACT.Silu).then_inc(*xc_ok.up())
                    act.wait_ge(*xdbl_ps.at(i, 2 * h + 1))
                    bcs = F[0:96, 9, 0:HALF].bitcast(BF16)
                    a.copy(bcs, ps[2][0:96, :]).then_inc(*bc_hi.up())
                    act.wait_ge(*xdbl_ps.at(i, 2 * h + 2))
                    a.copy(F[0:DT_RANK, 3, :], ps[3][0:DT_RANK, :]).then_inc(*dtlow_ok.up())
                    act.wait_ge(*dtp_ps.at(i, h + 1))
                    a.activation(f(4), ps[3][:], ACT.Abs, bias=bdt).then_inc(*sp_in.up())
                    a.activation(f(6), ps[3][:], ACT.Relu, bias=bdt).then_inc(*dtp_read.up())
                    act.wait_ge(*sp_in.at(i, h + 1))
                    a.activation(f(4), f(4), ACT.Exp, scale=-1.0).then_inc(*sp_exp.up())
                    act.wait_ge(*sp_exp.at(i, h + 1))
                    a.activation(f(5), f(4), ACT.Ln, bias=1.0).then_inc(*sp_ln.up())
                    act.wait_ge(*dt_ok.at(i, h + 1))
                    for n in range(N_STATE):
                        if n >= 2:
                            act.wait_ge(*scan_ok.at(i, N_STATE * h + n - 1))
                        a.activation(f(10 + n % 2), f(6), ACT.Exp, scale=negA[:, n:n + 1]).then_inc(*dA_ok.up())
                act.wait_ge(*var_ok.at(i, 2))
                rstd(small[:, 20:21], small[:, 19:20], i).then_inc(*rstd_ok.up())
                act.wait_ge(*aff_ok.at(i, 1))
                a.activation(f(0), ps[0][:], ACT.Silu, bias=small[:, 22:23], scale=small[:, 21:22]).then_inc(*gns_ok.up())
                layer_norm(0, i)
                act.wait_ge(*lin_ps.at(i, 1))
                a.activation(f(1), ps[2][:], ACT.Identity, bias=bk).then_inc(*lk_ok.up())
                layer_norm(1, i)
                act.wait_ge(*ln_ok.at(i, 2))
                for c in range(2):
                    last = a.copy(F[:, 1, HALF * c:HALF * c + HALF].rearrange("p (j s) -> p j s", j=4),
                                  bass.AP(upad, 2 + c + 2 * (P - 1), [[2 + L, P], [2 * P, 4], [-2, P]]))
                last.then_inc(*urev_ok.up())
                act.wait_ge(*uT_ps.at(i, 1))
                a.copy(f(0), ps[2][:]).then_inc(*uT_ok.up())
                for m in range(0, 4 * FILTERS, 2):
                    act.wait_ge(*conv_ps.at(i, m + 1))
                    if m >= 4:
                        act.wait_ge(*conv_used.at(i, m - 3))
                    a.copy(F[:, 4 + m % 4, 0:HALF], ps[2 + m % 4 // 2][:, HALF * (m % 2):HALF * (m % 2) + HALF]).then_inc(*conv_a.up())
                layer_norm(2, i)
                for n in range(3):
                    act.wait_ge(*qkv_ps.at(i, n + 1))
                    a.copy(f(n), ps[2 + n % 2][:]).then_inc(*qkv_ok.up())
                for m in range(GROUPS + 1):
                    if m < GROUPS:
                        n = P * (m % BLK + 1)
                        act.wait_ge(*negmax.at(i, m + 1))
                        if m >= 2:
                            act.wait_ge(*pT_ps.at(i, m - 1))
                        a.activation(F[:, 3 + m % 2, 0:n], ps[m % 2][:, 0:n], ACT.Exp, bias=small[:, 26 + 2 * (m % 2):27 + 2 * (m % 2)],
                                     scale=SCORE_SCALE, accum_out=small[:, 30 + m % 2:31 + m % 2]).then_inc(*probs.up())
                    if m >= 1:
                        n = P * ((m - 1) % BLK + 1)
                        act.wait_ge(*pT_ps.at(i, m))
                        if m >= 3:
                            act.wait_ge(*ctx_ps.at(i, m - 2))
                        a.copy(F[:, 5 + (m - 1) % 2, 0:n], ps[2 + (m - 1) % 2][:, 0:n]).then_inc(*pT_ok.up())
                layer_norm(3, i)
                act.wait_ge(*top_in.at(i, 1))
                a.activation(rtop[:, 2, :], rtop[:, 2, :], ACT.Exp).then_inc(*top_exp.up())
                act.wait_ge(*gateT_ps.at(i, 1))
                a.copy(F[0:2 * EXPERTS, 0, :], ps[3][0:2 * EXPERTS, :]).then_inc(*gateT_ok.up())
            assert astep.raised == ACT_STEPS, f"ACT_STEPS = {astep.raised}"

        @block.tensor
        def _(pe):
            def mm(o, w, r, start=True, stop=True):
                return t.matmul(o, w, r, start=start, stop=stop)

            def wide(o, w, r, start=True, stop=True):
                for q in range(2):
                    s = slice(HALF * q, HALF * q + HALF)
                    last = mm(o[:, s], w, r[:, s], start, stop)
                return last

            def layer_norm(n, i):
                pe.wait_ge(*ln_x.at(i, n + 1))
                wide(ps[0], mean64, X).then_inc(*ln_mean.up())
                pe.wait_ge(*ln_sq.at(i, n + 1))
                wide(ps[1], mean64, f(13)).then_inc(*ln_var.up())
                pe.wait_ge(*ln_ok.at(i, n + 1))

            pe.wait_ge(*ready.at(0, 1))
            with pe.Fori(0, PAIRS) as i:
                pe.wait_ge(*stat_in.at(i, 1))
                pe.wait_ge(*out_ok.at(i, 0))
                mm(ps[0][:, 0:2], mean2, small[:, 16:18]).then_inc(*stat_out.up())
                pe.wait_ge(*xn_ok.at(i, 1))
                for n in range(BLK):
                    tile = xpad[:, 1, 1 + 4 * n:5 + 4 * n, :].rearrange("p y x -> p (y x)")
                    last = t.transpose(ps[0][:, P * n:P * n + P], tile, ident)
                last.then_inc(*xnT_ps.up())
                for n in range(BLK):
                    for k in range(TAPS):
                        patch = xpad[:, k % 3, 4 * n + k // 3:4 * n + k // 3 + 4, :].rearrange("p y x -> p (y x)")
                        last = mm(ps[1][:, 36 * n:36 * n + 36], patch, woff[:, k, :, :].rearrange("p b o -> p (b o)"),
                                  k == 0, k == TAPS - 1)
                last.then_inc(*off_ps.up())
                for m in range(GROUPS + 1):
                    if m < GROUPS:
                        pe.wait_ge(*sample_ok.at(i, m + 1))
                        if m >= 2:
                            pe.wait_ge(*sampleT.at(i, m - 1))
                        sm = samples[m % 2][:].rearrange("p k c -> p (k c)")
                        for kk in range(KTILES):
                            n = P if kk < KTILES - 1 else C
                            last = t.transpose(ps[2 + m % 2][0:n, P * kk:P * kk + P], sm[:, P * kk:P * kk + n], ident)
                        last.then_inc(*sample_ps.up())
                    if m >= 4 and m % 4 == 0:
                        q = m // 4 - 1
                        h, tq = q // 2, q % 2
                        pe.wait_ge(*sampleT.at(i, 4 * q + 4))
                        if q == 0:
                            pe.wait_ge(*xnT_ok.at(i, 1))
                        st = F[:, 2 + 3 * (q % 2):5 + 3 * (q % 2), :].rearrange("p n l -> p (n l)")[:, 0:KTILES * HALF].rearrange("p (k q) -> p k q", k=KTILES)
                        for kk in range(KTILES):
                            n = P if kk < KTILES - 1 else C
                            last = mm(ps[0][:, HALF * tq:HALF * tq + HALF], wmain[0:n, kk, h, :], st[0:n, kk, :],
                                      h == 0 and kk == 0, h == 1 and kk == KTILES - 1)
                        last.then_inc(*conv_q.up())
                for h in range(2):
                    pe.wait_ge(*x1_ok.at(i, 1))
                    if h == 1:
                        pe.wait_ge(*hc_ok.at(i, N_STATE))
                    wide(ps[0], win[:, h, 0:P], X).then_inc(*xz_ps.up())
                    wide(ps[1], win[:, h, P:2 * P], X).then_inc(*xz_ps.up())
                    pe.wait_ge(*xc_ok.at(i, h + 1))
                    wide(ps[2][0:96, :], wxbc[:], f(2)).then_inc(*xdbl_ps.up())
                    if h == 1:
                        pe.wait_ge(*y2_ok.at(i, 1))
                    wide(ps[3][0:DT_RANK, :], wxdt[:], f(2)).then_inc(*xdbl_ps.up())
                    pe.wait_ge(*dtlow_ok.at(i, h + 1))
                    wide(ps[3], wdt[:], F[0:DT_RANK, 3, :]).then_inc(*dtp_ps.up())
                    pe.wait_ge(*bc_ok.at(i, h + 1))
                    bcs = F[0:96, 9, 0:HALF].bitcast(BF16)
                    for n in range(N_STATE + 1):
                        if n < N_STATE:
                            for b in range(2):
                                m = 2 * n + b
                                if b == 0 and n >= 2:
                                    pe.wait_ge(*hc_ok.at(i, N_STATE * h + n - 1))
                                if b == 1 and n >= 1:
                                    pe.wait_ge(*bin_ok.at(i, N_STATE * h + n))
                                wide(ps[m % 3], sel[:, N_STATE * b + n, :], bcs).then_inc(*bcast.up())
                        if n == 0:
                            pe.wait_ge(*dtp_read.at(i, h + 1))
                        else:
                            pe.wait_ge(*hc_ok.at(i, N_STATE * h + n))
                            wide(ps[3], ident, f(14 + (n - 1) % 2), n == 1, n == N_STATE).then_inc(*ysum.up())
                pe.wait_ge(*y2_ok.at(i, 2))
                for q in range(2):
                    s = slice(HALF * q, HALF * q + HALF)
                    for h in range(2):
                        last = mm(ps[0][:, s], wout[:, h, :], F[:, 16 + h, s], h == 0, h == 1)
                last.then_inc(*mout_ps.up())
                pe.wait_ge(*stat_in.at(i, 2))
                mm(ps[1][:, 0:2], mean16, small[:, 16:18]).then_inc(*stat_out.up())
                layer_norm(0, i)
                wide(ps[2], wqkv2[:, 1, :], upad[:, 2:]).then_inc(*lin_ps.up())
                wide(ps[3], wqkv2[:, 2, :], upad[:, 2:]).then_inc(*lin_ps.up())
                wide(ps[0], wqkv2[:, 0, :], upad[:, 2:]).then_inc(*lin_ps.up())
                layer_norm(1, i)
                pe.wait_ge(*urev_ok.at(i, 1))
                for n in range(BLK):
                    last = t.transpose(ps[2][:, P * n:P * n + P], F[:, 1, P * n:P * n + P], ident)
                last.then_inc(*uT_ps.up())
                pe.wait_ge(*uT_ok.at(i, 1))
                uT = f(0).rearrange("p (n c) -> p n c", c=P)

                def mix(m):
                    k, ap, odd = m // 4, m // 2 % 2, m % 2
                    for h in range(2):
                        r = slice(C * h, C * h + C)
                        for s0, s1, sg in SEGMENTS:
                            last = t.matmul(ps[h][r, HALF * ap + s0:HALF * ap + s1], mspec[r, sg, odd, k, :],
                                            F[r, 4 + m % 4, s0:s1], start=False, stop=False, skip_group_check=True)
                    last.then_inc(*conv_used.up())

                for m in range(4 * FILTERS + 1):
                    if m < 4 * FILTERS:
                        k, ap, odd = m // 4, m // 2 % 2, m % 2
                        src = ap ^ odd
                        lag = 1 if not (odd and ap == 0) else 0
                        if m % 4 == 0:
                            pe.wait_ge(*toep_in[k % 2].at(i, 16 * (k // 2 + 1)))
                        if m >= 4:
                            pe.wait_ge(*(conv_a if m % 2 == 0 else conv_v).at(i, m // 2 - 1))
                        slot = ps[2 + m % 4 // 2]
                        for j in range(4):
                            n = HALF - P * j
                            if m >= 1 and j == 3:
                                pe.wait_ge(*(conv_v if m % 2 == 0 else conv_a).at(i, (m - 1) // 2 + 1))
                            last = mm(slot[:, HALF * (m % 2) + P * j:HALF * (m % 2) + HALF], uT[:, 4 * src + j, :],
                                      toep[k % 2][:, odd, lag:lag + n], j == 0, j == 3)
                        last.then_inc(*conv_ps.up())
                    if m == 0:
                        xpar = X[:].rearrange("p (t a) -> p a t", a=2)
                        for h in range(2):
                            r = slice(C * h, C * h + C)
                            for ap in range(2):
                                t.matmul(ps[h][r, HALF * ap:HALF * ap + HALF], ident[r, r], xpar[r, ap, :], start=True, stop=True)
                    if m == 4 * FILTERS:
                        pe.wait_ge(*conv_v.at(i, 2 * FILTERS))
                        mm(ps[2][:, 0:2], ident, ident[:, 0:2])
                    if m >= 1:
                        mix(m - 1)
                for ap in range(2):
                    for h in range(2):
                        r = slice(C * h, C * h + C)
                        for s0, s1, sg in SEGMENTS:
                            for tap in range(3):
                                o = 2 + ap - tap + 2 * s0
                                last = t.matmul(ps[h][r, HALF * ap + s0:HALF * ap + s1], mar[r, sg, tap, :],
                                                upad[r, o:o + 2 * (s1 - s0) - 1:2], start=False, stop=False,
                                                skip_group_check=True)
                last.then_inc(*stu_ps.up())
                layer_norm(2, i)
                wide(ps[2], wqkv3[:, 0, :], upad[:, 2:]).then_inc(*qkv_ps.up())
                wide(ps[3], wqkv3[:, 1, :], upad[:, 2:]).then_inc(*qkv_ps.up())
                pe.wait_ge(*qkv_ok.at(i, 1))
                for n in range(BLK):
                    last = mm(ps[2][:, P * n:P * n + P], upad[:, 2 + P * n:2 + P * n + P], wqkv3[:, 2, :])
                last.then_inc(*qkv_ps.up())
                pe.wait_ge(*qkv_ok.at(i, 3))
                vtok = f(2).rearrange("p (n c) -> p n c", c=P)
                for m in range(GROUPS + 2):
                    if m < GROUPS:
                        h, qb = m // BLK, m % BLK
                        r = slice(C * h, C * h + C)
                        if m >= 2:
                            pe.wait_ge(*ctx_ok.at(i, m - 1))
                        n = P * (qb + 1)
                        for s0 in range(0, n, HALF):
                            s1 = min(n, s0 + HALF)
                            last = mm(ps[m % 2][:, s0:s1], F[r, 0, P * qb:P * qb + P], F[r, 1, s0:s1])
                        last.then_inc(*score_ps.up())
                    if 1 <= m <= GROUPS:
                        j = m - 1
                        pe.wait_ge(*probs.at(i, j + 1))
                        if j >= 2:
                            pe.wait_ge(*pT_ok.at(i, j - 1))
                        for n in range(j % BLK + 1):
                            last = t.transpose(ps[2 + j % 2][:, P * n:P * n + P], F[:, 3 + j % 2, P * n:P * n + P], ident)
                        last.then_inc(*pT_ps.up())
                    if m >= 1 and m <= GROUPS:
                        j = m - 1
                        h, qb = j // BLK, j % BLK
                        pe.wait_ge(*pT_ok.at(i, j + 1))
                        for n in range(qb + 1):
                            last = mm(ps[j % 2][:, 0:C], F[:, 5 + j % 2, P * n:P * n + P], vtok[:, n, C * h:C * h + C],
                                      n == 0, n == qb)
                        last.then_inc(*ctx_ps.up())
                pe.wait_ge(*ctx_ok.at(i, GROUPS))
                for n in range(BLK):
                    last = t.transpose(ps[2][:, P * n:P * n + P], F[:, 7, P * n:P * n + P], ident)
                last.then_inc(*ctxT_ps.up())
                layer_norm(3, i)
                for n in range(BLK):
                    last = mm(ps[2][:, 16 * n:16 * n + 16], upad[:, 2 + P * n:2 + P * n + P],
                              wrouter[:].rearrange("p b e -> p (b e)"))
                last.then_inc(*log_ps.up())
                pe.wait_ge(*gate_ok.at(i, 1))
                gates = route[:, 11, :, :].rearrange("p g e -> p (g e)")
                for n in range(BLK):
                    last = t.transpose(ps[3][0:16, P * n:P * n + P], gates[:, 16 * n:16 * n + 16], ident)
                last.then_inc(*gateT_ps.up())
                for m in range(GROUPS):
                    n, h = m // 2, m % 2
                    r = slice(C * h, C * h + C)
                    if m >= 2:
                        pe.wait_ge(*exp_read.at(i, m - 1))
                    mm(ps[0][:, HALF * h:HALF * h + HALF], upad[r, 2 + P * n:2 + P * n + P],
                       wexp[r, :, :].rearrange("p e c -> p (e c)")).then_inc(*exp_ps.up())
                pe.wait_ge(*gateT_ok.at(i, 1))
                for n in range(BLK):
                    pe.wait_ge(*moe_ok.at(i, 2 * n + 2))
                    s = slice(P * n, P * n + P)
                    mm(ps[1][:, s], bexp[:], F[0:2 * EXPERTS, 0, s], True, False)
                    last = mm(ps[1][:, s], F[:, 8, s], ident, False, True)
                last.then_inc(*moe_ps.up())

        @block.vector
        def _(dve):
            boot = lambda ins: (ins.then_inc(*boot_v.up()), dve.wait_ge(*boot_v.at(0, boot_v.raised)))
            based = [s for _, s in signals if s.base]
            for tile in (woff, wmain, win, wout, wqkv2, wqkv3, wrouter, bexp, xpad):
                last = v.memset(tile[:], 0.0)
                if based:
                    last.then_inc(based.pop().sem, 1)
            v.memset(eps, 1.0e-5)
            v.memset(upad[:, 0:2], 0.0).then_inc(*zeroed.up())
            v.memset(F[:, 9:11, :], 0.0).then_inc(*boot_s.up())
            dve.wait_ge(*mraw_in.at(0, 16 * 9))
            mw = lambda n, k=4: mixw[:, n:n + k]
            boot(v.tensor_tensor(mw(8), mw(0), mw(4), ALU.add))
            boot(v.tensor_reduce(mw(16, 1), mw(8), AX.X, ALU.max))
            boot(v.tensor_scalar(mw(8), mw(8), mw(16, 1), None, ALU.subtract))
            dve.wait_ge(*loaded.at(0, loaded.raised))
            boot(v.tensor_scalar(negA[:], negA[:], 80.0, None, ALU.min))
            dve.wait_ge(*boot_a.at(0, 3))
            boot(v.tensor_reduce(mw(17, 1), mw(12), AX.X, ALU.add))
            boot(v.reciprocal(mw(18, 1), mw(17, 1)))
            boot(v.tensor_scalar(mw(20), mw(12), mw(18, 1), None, ALU.mult))
            boot(v.tensor_reduce(mw(19, 1), mw(20), AX.X, ALU.max))
            boot(v.tensor_scalar(mw(24), mw(20), mw(19, 1), None, ALU.is_ge))
            dve.wait_ge(*loaded.at(0, loaded.raised))
            boot(v.tensor_tensor(mw(24), mw(24), cst[:, 5 * P + 100:5 * P + 104], ALU.mult))
            boot(v.tensor_reduce(mw(19, 1), mw(24), AX.X, ALU.max))
            boot(v.tensor_scalar(mw(24), mw(24), mw(19, 1), None, ALU.is_equal))
            boot(v.tensor_tensor(mw(24), mw(24), mw(20), ALU.subtract))
            boot(v.tensor_tensor(mw(24), mw(24), mw(20), ALU.add))
            dve.wait_ge(*boot_a.at(0, 2))
            flat = lambda a0: F[:, a0, :].rearrange("p (k e) -> p k e", e=C)
            sbc = spow[:].unsqueeze(2).broadcast_to([P, FILTERS, C])
            for e in range(STU_EXPERTS):
                sg = 3 - e
                for odd in range(2):
                    tmp = flat(11 + odd)
                    boot(v.tensor_tensor(tmp, flat(e), flat(4 + e), ALU.subtract if odd else ALU.add))
                    boot(v.tensor_tensor(tmp, tmp, sbc, ALU.mult))
                    if e == 0:
                        boot(v.tensor_scalar(mspec[:, sg, odd, :, :], tmp, mw(24, 1), None, ALU.mult))
                    else:
                        boot(v.scalar_tensor_tensor(out=mspec[:, sg, odd, :, :].rearrange("p k e -> p (k e)"), in0=F[:, 11 + odd, :],
                                                    scalar=mw(24 + e, 1), in1=mspec[:, sg + 1, odd, :, :].rearrange("p k e -> p (k e)"),
                                                    op0=ALU.mult, op1=ALU.add))
                mu = F[:, 8, 3 * C * e:3 * C * e + 3 * C]
                ma = mar[:, sg, :, :].rearrange("p r e -> p (r e)")
                if e == 0:
                    boot(v.tensor_scalar(ma, mu, mw(24, 1), None, ALU.mult))
                else:
                    boot(v.scalar_tensor_tensor(out=ma, in0=mu, scalar=mw(24 + e, 1),
                                                in1=mar[:, sg + 1, :, :].rearrange("p r e -> p (r e)"), op0=ALU.mult, op1=ALU.add))
            dve.wait_ge(*boot_a.at(0, 4))
            boot(v.tensor_scalar(negA[:], negA[:], -1.0, None, ALU.mult))
            dve.wait_ge(*tabled.at(0, 64))
            v.tensor_copy(sel[:], pick[0:96, :].unsqueeze(2).broadcast_to([96, 32, P])).then_inc(*ready.up())

            def link(ins, i):
                ins.then_inc(*vstep.up())
                dve.wait_ge(*vstep.at(i, vstep.raised))

            def group_stats(src, n, i):
                for q in range(2):
                    ins = v.bn_stats(small[:, 6 * q:6 * q + 6], src[:, HALF * q:HALF * q + HALF])
                ins.then_inc(*vstep.up())
                dve.wait_ge(*vstep.at(i, vstep.raised))
                v.tensor_copy(small[:, 40 + n:41 + n], eps)
                link(v.bn_aggr(small[:, 16:18], small[:, 0:12].rearrange("p (a b) -> p a b", a=2)), i)
                v.scalar_tensor_tensor(out=small[:, 17:18], in0=small[:, 16:17], scalar=small[:, 16:17], in1=small[:, 17:18],
                                       op0=ALU.mult, op1=ALU.add).then_inc(*stat_in.up())
                dve.wait_ge(*stat_out.at(i, n + 1))
                link(v.tensor_copy(small[:, 24:26], ps[n][:, 0:2]), i)
                link(v.scalar_tensor_tensor(out=small[:, 18:19], in0=small[:, 24:25], scalar=small[:, 24:25],
                                            in1=small[:, 25:26], op0=ALU.mult, op1=ALU.subtract), i)
                v.tensor_scalar(small[:, 19:20], small[:, 18:19], -1.0, 1.0e-5, ALU.mult, ALU.add).then_inc(*var_ok.up())
                dve.wait_ge(*rstd_ok.at(i, n + 1))

            def layer_norm(n, i):
                dve.wait_ge(*ln_mean.at(i, n + 1))
                v.tensor_tensor(f(12), X[:], ps[0][:], ALU.subtract).then_inc(*ln_cent.up())
                dve.wait_ge(*ln_rstd.at(i, n + 1))
                v.tensor_tensor(upad[:, 2:], f(12), f(13), ALU.mult).then_inc(*ln_ok.up())

            with dve.Fori(0, PAIRS) as i:
                vstep.raised = 0

                def dwait(n):
                    if dbg:
                        dve.wait_ge(*dbg_in.at(i, 16 * n))
                dve.wait_ge(*xin_in.at(i, 16))
                group_stats(xin, 0, i)
                image = xin[:].rearrange("p (y x) -> p y x", y=H)
                for dst, src in ((slice(0, W), slice(0, W)), (slice(1, W), slice(0, W - 1)), (slice(0, W - 1), slice(1, W))):
                    tap = 1 + src.start - dst.start
                    last = v.tensor_scalar(xpad[:, tap, 1:1 + H, dst], image[:, :, src], small[:, 24:25],
                                           small[:, 20:21], ALU.subtract, ALU.mult)
                last.then_inc(*xn_ok.up())
                dve.wait_ge(*off_ps.at(i, 1))
                offs = F[:, 1, 0:288].rearrange("p (n b o) -> p n b o", n=BLK, b=2)
                ops = ps[1][:, 0:288].rearrange("p (n b o) -> p n b o", n=BLK, b=2)
                bo = boff[:].unsqueeze(1).broadcast_to([P, BLK, 18])
                for b in range(2):
                    ins = v.tensor_tensor(offs[:, :, b, :], ops[:, :, b, :], bo, ALU.add)
                link(ins, i)
                cd = lambda n: coord[:, n, :]
                cg = lambda n: coord[:, n, :].rearrange("p (g a k) -> p g a k", g=GROUPS, a=2)
                for b in range(2):
                    gb = slice(BLK * b, BLK * b + BLK)
                    v.tensor_copy(cg(0)[:, gb, 0, :], offs[:, :, b, 0:18:6])
                    ins = v.tensor_copy(cg(0)[:, gb, 1, :], offs[:, :, b, 1:6:2])
                link(ins, i)
                link(v.tensor_tensor(cg(0)[:, :, :, 1], cg(0)[:, :, :, 1], cg(0)[:, :, :, 0], ALU.add), i)
                link(v.tensor_tensor(cg(0)[:, :, :, 2], cg(0)[:, :, :, 2], cg(0)[:, :, :, 1], ALU.add), i)
                link(v.tensor_tensor(cd(1), cd(0), base.rearrange("p g a k -> p (g a k)"), ALU.add), i)
                link(v.tensor_scalar(cd(1), cd(1), 1.0, W * 0.5, ALU.add, ALU.mult), i)
                link(v.tensor_scalar(cd(1), cd(1), 0.5, -2.0, ALU.subtract, ALU.max), i)
                link(v.tensor_scalar(cd(1), cd(1), float(W + 1), None, ALU.min), i)
                link(v.tensor_copy(cd(2).bitcast(I32), cd(1)), i)
                link(v.tensor_copy(cd(3), cd(2).bitcast(I32)), i)
                link(v.tensor_tensor(cd(4), cd(3), cd(1), ALU.is_gt), i)
                link(v.tensor_tensor(cd(5), cd(3), cd(4), ALU.subtract), i)
                ws = wsplit[:].rearrange("p g a k s -> p (g a k) s")
                link(v.tensor_tensor(ws[:, :, 1], cd(1), cd(5), ALU.subtract), i)
                v.tensor_scalar(ws[:, :, 0], ws[:, :, 1], -1.0, 1.0, ALU.mult, ALU.add)
                fx = cg(5)[:, :, 0, :]
                link(v.tensor_scalar(cg(6)[:, :, 1, :], cg(5)[:, :, 1, :], float(SIDE), float(2 * SIDE + 2), ALU.mult, ALU.add), i)
                v.tensor_tensor(index[:].rearrange("p g (x y) -> p g x y", x=3), fx.unsqueeze(3).broadcast_to([P, GROUPS, 3, 3]),
                                cg(6)[:, :, 1, :].unsqueeze(2).broadcast_to([P, GROUPS, 3, 3]), ALU.add).then_inc(*index_ok.up())
                for k in range(CORNERS):
                    ins = v.tensor_tensor(cweight[:, :, k, :].rearrange("p g (x y) -> p g x y", x=3),
                                          wsplit[:, :, 0, :, k % 2].unsqueeze(3).broadcast_to([P, GROUPS, 3, 3]),
                                          wsplit[:, :, 1, :, k // 2].unsqueeze(2).broadcast_to([P, GROUPS, 3, 3]), ALU.mult)
                link(ins, i)
                for m in range(GROUPS):
                    s = slots[m % SLOTS]
                    dve.wait_ge(*gathered[m % SLOTS].at(i, 16 * TAPS * (m // SLOTS + 1)))
                    wb = cweight[:, m, :, :].rearrange("p a k -> p k a").unsqueeze(3).broadcast_to([P, TAPS, CORNERS, C])
                    link(v.tensor_tensor(s[:], s[:], wb, ALU.mult), i)
                    link(v.tensor_tensor(s[:, :, 0:2, :], s[:, :, 0:2, :], s[:, :, 2:4, :], ALU.add), i)
                    if m >= 2:
                        dve.wait_ge(*sample_ps.at(i, m - 1))
                    last = v.tensor_tensor(samples[m % 2][:], s[:, :, 0, :], s[:, :, 1, :], ALU.add)
                    last.then_inc(*sample_ok.up())
                dve.wait_ge(*conv_q.at(i, 4))
                v.scalar_tensor_tensor(out=X[:], in0=ps[0][:], scalar=bmain, in1=xin[:], op0=ALU.add, op1=ALU.add).then_inc(*x1_ok.up())
                dwait(1)

                for h in range(2):
                    dve.wait_ge(*xh_pre.at(i, h + 1))
                    v.scalar_tensor_tensor(out=F[:, 0, 1:], in0=ps[0][:, 0:L - 1], scalar=cw0, in1=F[:, 0, 1:],
                                           op0=ALU.mult, op1=ALU.add).then_inc(*conv2.up())
                    bcs = F[0:96, 9, 0:HALF].bitcast(BF16)
                    rest = F[0:C, 14, :]
                    dve.wait_ge(*bc_hi.at(i, h + 1))
                    link(v.tensor_tensor(rest, ps[2][0:C, :], bcs[0:C, :], ALU.subtract), i)
                    link(v.tensor_copy(bcs[0:C, :], rest), i)
                    v.tensor_tensor(bcs[0:32, :], rest[0:32, :], bcs[0:32, :], ALU.subtract).then_inc(*bc_ok.up())
                    dve.wait_ge(*sp_exp.at(i, h + 1))
                    link(v.tensor_scalar(f(7), f(4), 1.0, 1.0, ALU.add, ALU.subtract), i)
                    link(v.tensor_tensor(f(7), f(4), f(7), ALU.subtract), i)
                    dve.wait_ge(*dtp_read.at(i, h + 1))
                    link(v.tensor_tensor(f(6), f(6), f(7), ALU.add), i)
                    dve.wait_ge(*sp_ln.at(i, h + 1))
                    v.tensor_tensor(f(6), f(6), f(5), ALU.add).then_inc(*dt_ok.up())
                    dve.wait_ge(*dt_ok.at(i, h + 1))
                    link(v.tensor_tensor(f(7), f(6), f(2), ALU.mult), i)

                    def input_term(n):
                        m = 2 * N_STATE * h + 2 * n
                        dve.wait_ge(*bcast.at(i, m + 1))
                        v.tensor_tensor(f(12 + n % 2), f(7), ps[(2 * n) % 3][:], ALU.mult).then_inc(*bin_ok.up())

                    input_term(0)
                    for n in range(N_STATE):
                        m = 2 * N_STATE * h + 2 * n
                        dve.wait_ge(*dA_ok.at(i, N_STATE * h + n + 1))
                        dve.wait_ge(*bin_ok.at(i, N_STATE * h + n + 1))
                        v.tensor_tensor_scan(f(8), f(10 + n % 2), f(12 + n % 2), 0.0, ALU.mult, ALU.add).then_inc(*scan_ok.up())
                        dve.wait_ge(*scan_ok.at(i, N_STATE * h + n + 1))
                        dve.wait_ge(*bcast.at(i, m + 2))
                        if n >= 2:
                            dve.wait_ge(*ysum.at(i, N_STATE * h + n - 1))
                        v.tensor_tensor(f(14 + n % 2), f(8), ps[(2 * n + 1) % 3][:], ALU.mult).then_inc(*hc_ok.up())
                        if n + 1 < N_STATE:
                            input_term(n + 1)
                    dve.wait_ge(*ysum.at(i, N_STATE * h + N_STATE))
                    link(v.scalar_tensor_tensor(out=f(8), in0=f(2), scalar=dskip, in1=ps[3][:], op0=ALU.mult, op1=ALU.add), i)
                    dve.wait_ge(*stored.at(i, 0))
                    v.tensor_tensor(f(16 + h), f(8), f(1), ALU.mult).then_inc(*y2_ok.up())
                dve.wait_ge(*mout_ps.at(i, 1))
                group_stats(ps[0], 1, i)
                link(v.tensor_tensor(small[:, 21:22], small[:, 20:21], gamma, ALU.mult), i)
                link(v.tensor_tensor(small[:, 23:24], small[:, 24:25], small[:, 21:22], ALU.mult), i)
                v.tensor_tensor(small[:, 22:23], beta, small[:, 23:24], ALU.subtract).then_inc(*aff_ok.up())
                dve.wait_ge(*gns_ok.at(i, 1))
                v.tensor_tensor(X[:], X[:], f(0), ALU.add).then_inc(*ln_x.up())
                dwait(2)
                layer_norm(0, i)
                dve.wait_ge(*lin_ps.at(i, 3))
                dve.wait_ge(*lk_ok.at(i, 1))
                link(v.scalar_tensor_tensor(out=f(2), in0=ps[3][:], scalar=bv, in1=f(1), op0=ALU.add, op1=ALU.mult,
                                            accum_out=small[:, 32:33]), i)
                link(v.tensor_scalar(f(2), ps[0][:], bq, small[:, 32:33], ALU.add, ALU.mult), i)
                v.tensor_tensor(X[:], X[:], f(2), ALU.add).then_inc(*ln_x.up())
                dwait(3)
                layer_norm(1, i)
                for m in range(1, 4 * FILTERS, 2):
                    dve.wait_ge(*conv_ps.at(i, m + 1))
                    if m >= 4:
                        dve.wait_ge(*conv_used.at(i, m - 3))
                    v.tensor_copy(F[:, 4 + m % 4, 0:HALF], ps[2 + m % 4 // 2][:, HALF * (m % 2):HALF * (m % 2) + HALF]).then_inc(*conv_v.up())
                dve.wait_ge(*stu_ps.at(i, 1))
                for h in range(2):
                    r = slice(C * h, C * h + C)
                    last = v.tensor_copy(X[r, :].rearrange("p (t a) -> p a t", a=2), ps[h][r, :].rearrange("p (a t) -> p a t", a=2))
                last.then_inc(*ln_x.up())
                dwait(4)
                layer_norm(2, i)
                for m in range(GROUPS + 1):
                    if m < GROUPS:
                        qb = m % BLK
                        n = P * (qb + 1)
                        sc = ps[m % 2]
                        nm = 26 + 2 * (m % 2)
                        dve.wait_ge(*score_ps.at(i, m + 1))
                        link(v.tensor_tensor(sc[:, n - P:n], sc[:, n - P:n], mask, ALU.add), i)
                        link(v.tensor_reduce(small[:, nm + 1:nm + 2], sc[:, 0:n], AX.X, ALU.max), i)
                        v.tensor_scalar(small[:, nm:nm + 1], small[:, nm + 1:nm + 2], -SCORE_SCALE, None, ALU.mult).then_inc(*negmax.up())
                    if m >= 1:
                        j = m - 1
                        h, qb = j // BLK, j % BLK
                        dve.wait_ge(*ctx_ps.at(i, j + 1))
                        link(v.reciprocal(small[:, 34 + j % 2:35 + j % 2], small[:, 30 + j % 2:31 + j % 2]), i)
                        v.tensor_scalar(F[:, 7, P * qb + C * h:P * qb + C * h + C], ps[j % 2][:, 0:C], small[:, 34 + j % 2:35 + j % 2],
                                        None, ALU.mult).then_inc(*ctx_ok.up())
                dve.wait_ge(*ctxT_ps.at(i, 1))
                v.tensor_tensor(X[:], X[:], ps[2][:], ALU.add).then_inc(*ln_x.up())
                dwait(5)
                layer_norm(3, i)
                dve.wait_ge(*log_ps.at(i, 1))
                rt = lambda n: route[:, n, :, :]
                top = lambda n: rtop[:, n, :]
                wide8 = lambda ap: ap.unsqueeze(2).broadcast_to([P, GROUPS, EXPERTS])
                perg = lambda ap: ap.unsqueeze(1).broadcast_to([P, GROUPS, EXPERTS])
                link(v.tensor_tensor(rt(0), ps[2][:, 0:P].rearrange("p (g e) -> p g e", e=EXPERTS), perg(brouter[:]), ALU.add), i)
                for r in range(2):
                    lg = rt(0) if r == 0 else rt(4)
                    link(v.tensor_reduce(top(r), lg, AX.X, ALU.max), i)
                    link(v.tensor_tensor(rt(1), lg, wide8(top(r)), ALU.is_ge), i)
                    link(v.tensor_tensor(rt(1), rt(1), perg(rank), ALU.mult), i)
                    link(v.tensor_reduce(top(3), rt(1), AX.X, ALU.max), i)
                    link(v.tensor_tensor(rt(2 + r), rt(1), wide8(top(3)), ALU.is_equal), i)
                    if r == 0:
                        link(v.tensor_scalar(rt(5), rt(2), -1.0e30, None, ALU.mult), i)
                        link(v.tensor_tensor(rt(4), rt(0), rt(5), ALU.add), i)
                v.tensor_tensor(top(2), top(1), top(0), ALU.subtract).then_inc(*top_in.up())
                dve.wait_ge(*top_exp.at(i, 1))
                link(v.tensor_scalar(top(4), top(2), 1.0, None, ALU.add), i)
                link(v.reciprocal(top(4), top(4)), i)
                link(v.tensor_tensor(top(5), top(4), top(2), ALU.mult), i)
                link(v.tensor_tensor(rt(6), rt(2), wide8(top(4)), ALU.mult), i)
                link(v.tensor_tensor(rt(7), rt(3), wide8(top(5)), ALU.mult), i)
                v.tensor_tensor(rt(11), rt(6), rt(7), ALU.add).then_inc(*gate_ok.up())
                dve.wait_ge(*gate_ok.at(i, 1))
                mo = f(8).rearrange("p (n b c) -> p n b c", n=BLK, b=2)
                for m in range(GROUPS):
                    n, h = m // 2, m % 2
                    dve.wait_ge(*exp_ps.at(i, m + 1))
                    if m >= 2:
                        dve.wait_ge(*moe_ok.at(i, m - 1))
                    tmp = F[:, 9 + h, 0:HALF].rearrange("p (e c) -> p e c", c=C)
                    v.tensor_tensor(tmp, ps[0][:, HALF * h:HALF * h + HALF].rearrange("p (e c) -> p e c", c=C),
                                    route[:, 11, m, :].unsqueeze(2).broadcast_to([P, EXPERTS, C]), ALU.mult).then_inc(*exp_read.up())
                    dve.wait_ge(*exp_read.at(i, m + 1))
                    v.tensor_reduce(mo[:, n, h, :], tmp.rearrange("p e c -> p c e"), AX.X, ALU.add).then_inc(*moe_ok.up())
                dve.wait_ge(*moe_ps.at(i, 1))
                v.tensor_tensor(f(17), X[:], ps[1][:], ALU.add).then_inc(*out_ok.up())
            assert vstep.raised == DVE_STEPS, f"DVE_STEPS = {vstep.raised}"

        wrong = [(n, s.raised, s.per_pair) for n, s in signals if s.per_pair and s.raised and s.raised != s.per_pair]
        assert not wrong, wrong


def arrays_of(i):
    n = {k: np.asarray(w) for k, w in i.items()}
    phi = n["L2_ffn_phi"][:L]
    phi_pad = np.zeros((FILTERS, 2, P + HALF), phi.dtype)
    phi_pad[:, 0, P:] = phi[0::2].T
    phi_pad[:, 1, P:] = phi[1::2].T
    return {
        "x": n["x"], "consts": shape_constants(),
        "w_off": n["L0_conv_w_off"].transpose(1, 2, 3, 0).reshape(C, TAPS, 18), "b_off": n["L0_conv_b_off"],
        "w_main": n["L0_conv_w_main"].reshape(C, C, TAPS).transpose(2, 1, 0), "b_main": n["L0_conv_b_main"],
        "W_in": n["L1_conv_W_in"], "conv_w": n["L1_conv_conv_w"], "conv_b": n["L1_conv_conv_b"],
        "W_x": n["L1_conv_W_x"], "W_dt": n["L1_conv_W_dt"], "b_dt": n["L1_conv_b_dt"],
        "A_log": n["L1_conv_A_log"], "D": n["L1_conv_D"], "W_out": n["L1_conv_W_out"],
        "gn_gamma": n["L1_conv_gn_gamma"], "gn_beta": n["L1_conv_gn_beta"],
        "Wq2": n["L2_attn_Wq"], "bq2": n["L2_attn_bq"], "Wk2": n["L2_attn_Wk"], "bk2": n["L2_attn_bk"],
        "Wv2": n["L2_attn_Wv"], "bv2": n["L2_attn_bv"], "sigma": n["L2_ffn_sigma"], "phi_pad": phi_pad,
        "M_u": n["L2_ffn_M_u"], "M_plus": n["L2_ffn_M_phi_plus"], "M_minus": n["L2_ffn_M_phi_minus"],
        "log_weights": n["L2_ffn_log_weights"], "gumbel": n["L2_ffn_gumbel"],
        "Wq3": n["L3_attn_Wq"], "Wk3": n["L3_attn_Wk"], "Wv3": n["L3_attn_Wv"],
        "router_w": n["L3_ffn_router_w"], "router_b": n["L3_ffn_router_b"],
        "expert_w": n["L3_ffn_expert_w"], "expert_b": n["L3_ffn_expert_b"],
    }


def build(nc, arrays, dbg=False):
    args = [nc.dram_tensor(f"in_{k}_dram", w.shape, mybir.dt.from_np(w.dtype), kind="ExternalInput").ap()
            for k, w in arrays.items()]
    tables = [nc.dram_tensor(f"corners{n}", [SIDE * SIDE, CORNERS * C], F32).ap() for n in range(2)]
    out = nc.dram_tensor("out_0_dram", [BATCH, C, H, W], F32, kind="ExternalOutput").ap()
    dbgs = [nc.dram_tensor(f"dbg{n}", [BATCH, C, H, W], F32, kind="ExternalOutput").ap() for n in range(5)] if dbg else None
    nc.disable_value_cache = True
    hybrid_kernel(nc, *args, tables, out, dbgs)


def kernel(**inputs):
    import concourse.bacc as bacc
    from concourse.bass_utils import run_bass_kernel_spmd

    arrays = {k: np.ascontiguousarray(w) for k, w in arrays_of(inputs).items()}
    nc = bacc.Bacc("TRN2", target_bir_lowering=False, num_devices=1)
    build(nc, arrays)
    r = run_bass_kernel_spmd(nc, [{f"in_{k}_dram": w for k, w in arrays.items()}], core_ids=[0])
    return r.results[0]["out_0_dram"]
```

```python
from contextlib import ExitStack

import numpy as np

import concourse.bass as bass
from concourse import mybir

F32 = mybir.dt.float32
BF16 = mybir.dt.bfloat16
I32 = mybir.dt.int32
U32 = mybir.dt.uint32
ALU = mybir.AluOpType
ACT = mybir.ActivationFunctionType
AX = mybir.AxisListType

P = 128
BATCH, C, H, W = 8, 64, 32, 32
L = H * W
PAIRS = BATCH // 2
BLK = L // P
TAPS = 9
KTILES = (TAPS + 1) // 2
SIDE = H + 4
CORNERS = 4
N_STATE = 16
DT_RANK = 4
FILTERS = 16
EXPERTS = 8
STU_EXPERTS = 4
HALF = L // 2
TOEP = HALF + 1
GROUPS = 2 * BLK
SLOTS = 4
NEG = -1.0e12
SCORE_SCALE = 1.0 / float(np.sqrt(L))
SEGMENTS = [(0, 64, 0), (64, 128, 1), (128, 256, 2), (256, 512, 3)]

STEPS_A = 49
STEPS_B = 18
STEPS_C = 2
STEPS_D = 66


class Signal:

    def __init__(self, sem, per_pair, base):
        self.sem, self.per_pair, self.base, self.raised = sem, per_pair, base, 0

    def up(self, n=1):
        self.raised += n
        return self.sem, n

    def at(self, i, n):
        return self.sem, i * self.per_pair + (n + self.base)


def shape_constants():
    r = np.arange(P)
    ident = np.eye(P)
    mean_of = lambda g: (r[:, None] // g == r[None, :] // g) / g
    mask = np.where(r[None, :] > r[:, None], NEG / SCORE_SCALE, 0.0)
    tok = np.arange(L).reshape(BLK, P)
    lin = np.linspace(-1.0, 1.0, H).astype(np.float32)
    base = np.zeros((P, 2, BLK, 2, 3))
    base[:, :, :, 0, :] = lin[tok % W].T[:, None, :, None]
    base[:, :, :, 1, :] = lin[tok // W].T[:, None, :, None]
    rank = np.broadcast_to(np.arange(EXPERTS, 0, -1), (P, EXPERTS))
    pick = (r[:, None] % 32 == np.arange(32)[None, :]) * 1.0
    parts = [ident, mean_of(2), mean_of(16), mean_of(64), mask, base.reshape(P, -1), rank, pick]
    return np.ascontiguousarray(np.concatenate(parts, 1).astype(np.float32))


def hybrid_kernel(nc, x, consts, w_off, b_off, w_main, b_main, W_in, conv_w, conv_b, W_x, W_dt, b_dt,
                  A_log, D, W_out, gn_gamma, gn_beta, Wq2, bq2, Wk2, bk2, Wv2, bv2, sigma, phi_pad,
                  M_u, M_plus, M_minus, log_weights, gumbel, Wq3, Wk3, Wv3, router_w, router_b,
                  expert_w, expert_b, tables, mixing, out):
    ctx = ExitStack()
    with ctx:
        def sb(name, shape, dt=F32):
            return ctx.enter_context(nc.sbuf_tensor(name, shape, dt))

        signals = []

        def sig(name, per_pair=0, base=0):
            s = Signal(ctx.enter_context(nc.semaphore(name)), per_pair, base)
            signals.append((name, s))
            return s

        v, a, g, t = nc.vector, nc.scalar, nc.gpsimd, nc.tensor

        cst = sb("cst", [P, consts.shape[1]])
        ident, mean2, mean16, mean64, mask = (cst[:, P * n:P * n + P] for n in range(5))
        base = cst[:, 5 * P:5 * P + 96]
        rank = cst[:, 5 * P + 96:5 * P + 104]
        pick = cst[:, 5 * P + 104:5 * P + 136]
        woff = sb("woff", [P, 3, 96])
        wmain = sb("wmain", [P, KTILES, 2, P])
        win = sb("win", [P, 2, 4 * C])
        wxdt = sb("wxdt", [P, DT_RANK])
        wxbc = sb("wxbc", [P, 96])
        wdt = sb("wdt", [DT_RANK, P])
        wout = sb("wout", [P, 2, P])
        sel = sb("sel", [96, 32, P], BF16)
        negA = sb("negA", [P, N_STATE])
        wqkv2 = sb("wqkv2", [P, 3, P])
        wqkv3 = sb("wqkv3", [P, 3, P])
        wrouter = sb("wrouter", [P, 2, EXPERTS])
        wexp = sb("wexp", [P, EXPERTS, C])
        bexp = sb("bexp", [2 * EXPERTS, P])
        boff = sb("boff", [P, 18])
        brouter = sb("brouter", [P, EXPERTS])
        cols = sb("cols", [P, 12])
        (bmain, cw0, cw1, cb, bdt, dskip, gamma, beta, bq, bk, bv, eps) = (cols[:, n:n + 1] for n in range(12))
        mar = sb("mar", [P, 4, 3, P])
        mixw = sb("mixw", [P, 40])
        spow = sb("spow", [P, FILTERS])

        xin = sb("xin", [P, L])
        XF = sb("XF", [P, L])
        own_slots = sb("own_slots", [P, 2, TAPS * CORNERS * C])
        stream = sb("stream", [P, TAPS * CORNERS * C])
        samples = [sb(f"samples{n}", [P, TAPS, C]) for n in range(2)]
        coord = sb("coord", [P, 7, 96])
        wsplit = sb("wsplit", [P, GROUPS, 2, 3, 2])
        index = sb("index", [P, GROUPS, TAPS], U32)
        cweight = sb("cweight", [P, GROUPS, CORNERS, TAPS])
        sa = sb("sa", [P, 32])
        sbm = sb("sbm", [P, 32])
        sd = sb("sd", [P, 16])
        toep = [stream[:, 2 * TOEP * n:2 * TOEP * (n + 1)].rearrange("p (o m) -> p o m", o=2) for n in range(2)]
        lent = sb("lent", [P, 2 * L + 2 + 2 * 8 * P])
        XB = lent[:, 0:L]
        upad = lent[:, L:2 * L + 2]
        mring = [lent[:, 2 * L + 2 + 8 * P * n:2 * L + 2 + 8 * P * (n + 1)].rearrange("p (s c) -> p s c", s=8) for n in range(2)]
        route = sb("route", [P, 9, GROUPS, EXPERTS])
        rtop = sb("rtop", [P, 6, GROUPS])
        all_tiles = sb("all_tiles", [P, 22 * L + 192])
        F = all_tiles[:, 0:22 * L].rearrange("p (n l) -> p n l", l=L)

        def f(n):
            return F[:, n, :]

        SZ, XC, DT, DTX, Y = (0, 1), (2, 3), (4, 5), (6, 7), (17, 18)
        BCS, DA, DBX, HC, KV, HS = 8, (9, 10), (11, 12), (13, 14), 15, 16
        UT, RING = 19, 20
        Q, K, V, PR, PT, CTX, MO, TMP, LN0, LN1, OUT = 0, 1, 2, (3, 4), 5, 7, 8, 9, 11, 12, 16
        ST = 17

        ps = [ctx.enter_context(nc.psum_tensor(f"ps{n}", [P, L], F32)) for n in range(4)]

        class Places:

            def __init__(self, beside_b, ahead):
                wide_tiles = all_tiles[:, (19 if beside_b else ST) * L:]
                quarter = KTILES * HALF
                self.xpad = wide_tiles[:, 0:(H + 2) * W].rearrange("p (y x) -> p y x", x=W)
                st = (wide_tiles[:, 0:quarter], lent[:, 0:quarter] if beside_b else wide_tiles[:, quarter:2 * quarter])
                self.st = [w.rearrange("p (k q) -> p k q", k=KTILES) for w in st]
                self.xnT = lent[:, quarter:quarter + L] if beside_b else f(13)
                self.offT = F[0:96, 15 if beside_b else 14, :]
                places = [own_slots[:, 0, :], own_slots[:, 1, :], stream[:]]
                if not beside_b:
                    places += [all_tiles[:, 13 * L:13 * L + TAPS * CORNERS * C]]
                self.slots = [w.rearrange("p (k n c) -> p k n c", k=TAPS, c=C) for w in places]
                self.ps_mean, self.ps_xnT, self.ps_offT, self.ps_offs = ps[0], ps[1], ps[0], ps[0]
                self.ahead = ahead
                if ahead:
                    own = own_slots[:].rearrange("p a b -> p (a b)")
                    border = (H + 2) * W
                    self.xpad = own[:, 0:border].rearrange("p (y x) -> p y x", x=W)
                    self.xnT = own[:, border:border + L]
                    self.offT = F[0:96, 15, :]
                    self.ps_mean, self.ps_xnT, self.ps_offT, self.ps_offs = ps[2], ps[2], ps[2], ps[2]

            def slot(self, m):
                n = len(self.slots)
                if self.ahead:
                    return self.slots[m % 2 if m < n else (m - 2) % n], m - 2 if m < n else m - n if m >= n + 2 else -1
                return self.slots[m % n], m - n

        in_attention, beside_b, in_scan = Places(False, False), Places(True, False), Places(False, True)

        def places(ja):
            return in_scan if not isinstance(ja, int) else beside_b if ja == 1 else in_attention

        bcs = [F[0:96, BCS, HALF * h:HALF * h + HALF].bitcast(BF16) for h in range(2)]
        ring = [F[:, RING + n // 2, HALF * (n % 2):HALF * (n % 2) + HALF] for n in range(4)]
        pts = [F[:, PT + n // 2, HALF * (n % 2):HALF * (n % 2) + HALF] for n in range(4)]

        bank_conv = ps[0][:, 0:HALF]
        bank_t0, bank_t1 = ps[1][:, 0:HALF], ps[1][:, HALF:L]

        NS = 2 * N_STATE

        zeroed, loaded, tabled, mraw_in = sig("zeroed"), sig("loaded"), sig("tabled"), sig("mraw_in")
        boot_v, boot_a, ready, mspec_ok = sig("boot_v"), sig("boot_a"), sig("ready"), sig("mspec_ok")
        mixing_in, cleared, early, setup_done = sig("mixing_in"), sig("cleared"), sig("early"), sig("setup_done")
        RAW_LOADS = 7
        vA, vB, vC, vD = sig("vA", STEPS_A), sig("vB", STEPS_B), sig("vC", STEPS_C), sig("vD", STEPS_D)
        xin_in = sig("xin_in", 16)
        statA_in, statA_out, varA_ok, lnA_ok, rstdA_ok = (sig(n, 1) for n in ("statA_in", "statA_out", "varA_ok", "lnA_ok", "rstdA_ok"))
        xn_ok, xnT_ps, xnT_ok, off_ps = (sig(n, 1) for n in ("xn_ok", "xnT_ps", "xnT_ok", "off_ps"))
        off_read = sig("off_read", 1)
        offT_ps, offT_ok = sig("offT_ps", 2), sig("offT_ok", 2)
        table_in = sig("table_in", 16 * 32)
        pool_tick = sig("pool_tick", GROUPS, base=1)
        index_ok = sig("index_ok", 1)
        gathered = [sig(f"gathered{n}", 16 * TAPS * GROUPS // SLOTS) for n in range(SLOTS)]
        sample_ok = sig("sample_ok", GROUPS, base=1)
        sample_ps = sig("sample_ps", GROUPS)
        sampleT = sig("sampleT", GROUPS)
        sampleT4 = sig("sampleT4", 4)
        conv_q = sig("conv_q", 4)
        x1_ok = sig("x1_ok", 2)
        xcopy_ok = sig("xcopy_ok", 1)
        xz_ps = sig("xz_ps", 4)
        xh_pre, conv2, xc_ok, bc_hi, bc_ok, dtlow_ok = (sig(n, 2) for n in ("xh_pre", "conv2", "xc_ok", "bc_hi", "bc_ok", "dtlow_ok"))
        xdbl_ps = sig("xdbl_ps", 4)
        dtp_ps, sp_abs, dtp_read, sp_exp, sp_ln, dt_ok, dtx_ok = (sig(n, 2) for n in ("dtp_ps", "sp_abs", "dtp_read", "sp_exp", "sp_ln", "dt_ok", "dtx_ok"))
        dA_ok, scan_ok, b_ps, c_ps, bin_ok, hc_ok, ysum = (sig(n, NS) for n in ("dA_ok", "scan_ok", "b_ps", "c_ps", "bin_ok", "hc_ok", "ysum"))
        y2_ok = sig("y2_ok", 2)
        mout_ps, statB_in, statB_out, varB_ok, lnB_ok, rstdB_ok, aff_ok, gns_ok = (
            sig(n, 1) for n in ("mout_ps", "statB_in", "statB_out", "varB_ok", "lnB_ok", "rstdB_ok", "aff_ok", "gns_ok"))

        def spec_tile(sg, odd):
            return 9 + 2 * (sg % 2) + odd

        def first_pair(j):
            return isinstance(j, int) and j == 0

        def last_pair(j):
            return isinstance(j, int) and j == PAIRS - 1

        def late(j):
            return xin if last_pair(j) else XB

        def cpad(j):
            return own_slots[:, 0, 0:2 + L] if last_pair(j) else upad

        class LayerNorm:

            def __init__(self, name, src, dst, t0, t1, p0, p1):
                self.src, self.dst, self.t0, self.t1, self.p0, self.p1 = src, dst, t0, t1, p0, p1
                self.x, self.mean, self.cent, self.sq, self.var, self.ln, self.rstd, self.ok = (
                    sig(f"{name}_{n}", 1) for n in ("x", "mean", "cent", "sq", "var", "ln", "rstd", "ok"))

        lc1 = LayerNorm("lc1", lambda j: XF, cpad, RING, RING + 1, ps[0], ps[1])
        lc2 = LayerNorm("lc2", late, cpad, RING, RING + 1, ps[0], ps[1])
        ld1 = LayerNorm("ld1", late, lambda j: upad, LN0, LN1, ps[0], ps[1])
        ld2 = LayerNorm("ld2", late, lambda j: upad, LN0, LN1, ps[2], ps[3])
        lin_ps = sig("lin_ps", 3)
        lk_ok = sig("lk_ok", 1)
        urev_ok, uT_ps, uT_ok = (sig(n, 1) for n in ("urev_ok", "uT_ps", "uT_ok"))
        tiles_in = [sig(f"tiles_in{n}", 3 * 16 * FILTERS // 2) for n in range(2)]
        conv_ps = sig("conv_ps", 4 * FILTERS)
        conv_a = sig("conv_a", 2 * FILTERS)
        conv_v = sig("conv_v", 2 * FILTERS)
        conv_used = sig("conv_used", 4 * FILTERS, base=1)
        stu_ps = sig("stu_ps", 1)
        qkv_ps, qkv_ok = sig("qkv_ps", 3), sig("qkv_ok", 3)
        score_ps, negmax, probs, ctx_ok = (sig(n, GROUPS) for n in ("score_ps", "negmax", "probs", "ctx_ok"))
        chunks = [(j, b0, min(b0 + 4, j % BLK + 1)) for j in range(GROUPS) for b0 in range(0, j % BLK + 1, 4)]
        pT_ps, pT_ok, pv_done = (sig(n, len(chunks)) for n in ("pT_ps", "pT_ok", "pv_done"))
        ctxT_ps, log_ps, top_in, top_exp, gate_ok, gateT_ps, gateT_ok = (
            sig(n, 1) for n in ("ctxT_ps", "log_ps", "top_in", "top_exp", "gate_ok", "gateT_ps", "gateT_ok"))
        exp_ps, exp_read, moe_ok = (sig(n, GROUPS) for n in ("exp_ps", "exp_read", "moe_ok"))
        moe_ps = sig("moe_ps", 1)
        out_ok = sig("out_ok", 1, base=1)
        stored = sig("stored", 16, base=1)

        x_v = x.rearrange("(i b) c h w -> i (b c) (h w)", b=2)
        out_v = out.rearrange("(i b) c h w -> i (b c) (h w)", b=2)
        col_of = lambda w: w.rearrange("(p a) -> p a", a=1)
        row_of = lambda w: w.rearrange("(a p) -> a p", a=1)
        bcast_row = lambda w: row_of(w).broadcast_to([P, w.shape[0]])
        image = [slice(0, C), slice(C, P)]
        groups = [(h, 4 * tq + b) for tq in range(2) for h in range(2) for b in range(4)]

        def run(eng, scan, attention):
            attention(None, 0)
            scan(0, None, ja=1)
            with eng.Fori(1, PAIRS - 1) as j:
                scan(j, j - 1, jn=j + 1)
                attention(j - 1, j + 1)
            scan(PAIRS - 1, PAIRS - 2)
            scan(None, PAIRS - 1, jd=PAIRS - 2)
            attention(PAIRS - 1, None)

        SETUP_AT = 3
        AHEAD = 2
        GATES_AT = 2

        def attention_order(ja):
            started = AHEAD if ja is not None and places(ja).ahead else 0
            gathers = [[("gather", m)] + ([("turn", m - 1)] if m else []) for m in range(started, GROUPS)]
            gathers[-1] += [("turn", GROUPS - 1)]
            units = [("turn", m) for m in range(started - 1)]
            for q in range(GROUPS):
                units += [("query", q)] + (gathers.pop(0) if len(gathers) > 2 else []) + [("values", q)]
            units += [("router", 0)] + gathers.pop(0) + [("router", 1)] + [u for g in gathers for u in g] + [("router", 2)]
            return units + [("expert", m) for m in range(GROUPS)]

        FRONT = {2: "stats", 3: "average", 4: "shift", 5: "turn x", 6: "offsets 0", 7: "offsets 1", 8: "turn offsets"}
        POSITION_PARTS = 6
        TABLES_AT = 4
        FETCH_AT = {18: 0, 20: 1, 25: 2, 28: 3}
        GATHER_AT = {23: 0, 26: 1}

        def gather_share(s):
            units = []
            for m in range(GROUPS):
                if m and s == m * 9 // 5:
                    units += [("fetch", m)]
                if s == min(3 + m * 9 // 5, NS):
                    units += [("gather", m)] + ([("turn", m - 1)] if m else [])
            return units + ([("turn", GROUPS - 1)] if s == NS else [])

        def share(s):
            if s < GROUPS:
                return [("query", s), ("values", s)]
            return ([("router", n) for n in range(3)] if s == GROUPS else []) + [("expert", s - GROUPS)]


        block = ctx.enter_context(nc.Block())

        @block.sync
        def _(sp):
            def load(dst, src, s=loaded):
                sp.dma_start(dst, src).then_inc(*s.up(16))

            load(cst[:], consts, early)
            load(xin[:], x_v[0], xin_in)
            load(boff[:], bcast_row(b_off), early)
            sp.wait_ge(*zeroed.at(0, 1))
            for h, r in enumerate(image):
                load(F[r, 16, 0:TAPS * 18].rearrange("p (k o) -> p k o", o=18), w_off, early)
            for tb in tables:
                tv = tb.rearrange("r c -> (r c)").rearrange("(p q) -> p q", p=P)
                half = tv.shape[1] // 2
                for hh in range(2):
                    load(tv[:, half * hh:half * hh + half], lent[:, 2 * L + 2:2 * L + 2 + half], tabled)
            for tile, m in ((0, M_plus), (4, M_minus)):
                load(F[0:C, tile:tile + 4, :].rearrange("p n l -> p (n l)").rearrange("p (i k e) -> p i k e", i=4, e=C),
                     m.rearrange("i k d e -> d i k e"), mraw_in)
            for r in image:
                load(F[r, 8, 0:12 * C].rearrange("p (i r e) -> p i r e", i=4, e=C), M_u.rearrange("i r d e -> d i r e"), mraw_in)
            load(mixw[:, 0:4], bcast_row(log_weights), mraw_in)
            load(mixw[:, 4:8], bcast_row(gumbel), mraw_in)
            load(spow[:], bcast_row(sigma), mraw_in)
            assert mraw_in.raised == 16 * RAW_LOADS

            def load_rest():
                for h, r in enumerate(image):
                    for kk in range(KTILES):
                        for aa in range(2 if kk < KTILES - 1 else 1):
                            load(wmain[C * aa:C * aa + C, kk, h, r], w_main[2 * kk + aa])
                    load(win[r, h, :], W_in)
                    load(wout[:, h, r], W_out)
                    for n, w in enumerate((Wq2, Wk2, Wv2)):
                        load(wqkv2[r, n, r], w)
                    for n, w in enumerate((Wq3, Wk3, Wv3)):
                        load(wqkv3[r, n, r], w)
                    load(wrouter[r, h, :], router_w)
                    load(wexp[r, :, :], expert_w.rearrange("e d c -> d e c"))
                    load(bexp[EXPERTS * h:EXPERTS * h + EXPERTS, r], expert_b)
                    for dst, src in ((bmain, b_main), (gamma, gn_gamma), (beta, gn_beta), (bq, bq2), (bk, bk2), (bv, bv2)):
                        load(dst[r, :], col_of(src))
                for dst, src in ((cb, conv_b), (bdt, b_dt), (dskip, D)):
                    load(dst, col_of(src))
                load(cols[:, 1:3], conv_w)
                load(wxdt[:], W_x[:, 0:DT_RANK])
                for q in range(3):
                    load(wxbc[:, 32 * q:32 * q + 32], W_x[:, DT_RANK:])
                load(wdt[:], W_dt)
                load(negA[:], A_log)
                load(brouter[:], bcast_row(router_b))

            def store_mixing():
                for e in range(STU_EXPERTS):
                    sg = 3 - e
                    sp.wait_ge(*mspec_ok.at(0, e + 1))
                    for odd in range(2):
                        load(mixing[:, :, 2 * sg + odd, :].rearrange("k d e -> d k e"),
                             F[0:C, spec_tile(sg, odd), :].rearrange("p (k e) -> p k e", e=C), mixing_in)

            def store(jd):
                sp.wait_ge(*out_ok.at(jd, 1))
                load(out_v[jd], f(OUT), stored)

            def scan(jb, jc, jd=None, ja=None, jn=None):
                if jb is not None and (not isinstance(jb, int) or jb < PAIRS - 1):
                    sp.wait_ge(*xcopy_ok.at(jb, 1))
                    if jc is not None:
                        sp.wait_ge(*xz_ps.at(jb, 4))
                    load(xin[:], x_v[jb + 1], xin_in)
                if jc is not None:
                    if jb is not None:
                        sp.wait_ge(*x1_ok.at(jb, 2))
                    for k in range(FILTERS):
                        sp.wait_ge(*conv_used.at(jc, max(4 * (k - 1), 0)))
                        src = bass.AP(phi_pad.tensor, k * 2 * (P + HALF), [[1, P], [P + HALF, 2], [1, TOEP]])
                        load(toep[k % 2][:], src, tiles_in[k % 2])
                        for r in image:
                            load(mring[k % 2][r, :, r], mixing[k], tiles_in[k % 2])
                        if jn is not None and TABLES_AT <= k < TABLES_AT + 4:
                            write_tables(jn, [k - TABLES_AT])
                if jd is not None:
                    store(jd)
                if ja is not None:
                    write_tables(ja)
                    sp.wait_ge(*cleared.at(0, 1))

            def write_tables(ja, corners=range(CORNERS)):
                if ja is not None:
                    sp.wait_ge(*xnT_ok.at(ja, 1))
                    xnT = places(ja).xnT.rearrange("p (n c) -> p n c", n=BLK)
                    for h in range(2):
                        tb = tables[h].rearrange("(y x) (k c) -> y x k c", x=SIDE, c=C)
                        for k in corners:
                            dy, dx = k // 2, k % 2
                            for yy in range(4):
                                dst = tb[2 - dy + yy:2 - dy + yy + 4 * (BLK - 1) + 1:4, 2 - dx:2 - dx + W, k, :]
                                load(dst.rearrange("n x c -> x n c"), xnT[32 * yy:32 * yy + 32, :, C * h:C * h + C], table_in)

            def attention(jd, ja):
                if ja is not None and not places(ja).ahead:
                    write_tables(ja)
                if first_pair(ja):
                    load_rest()
                    store_mixing()
                    sp.wait_ge(*mixing_in.at(0, 16 * 2 * STU_EXPERTS))
                if jd is not None:
                    store(jd)

            sp.wait_ge(*tabled.at(0, 64))
            run(sp, scan, attention)
            sp.wait_ge(*stored.at(PAIRS - 1, 16))
            for s in (table_in,):
                sp.wait_ge(*s.at(PAIRS - 1, s.per_pair))

        @block.gpsimd
        def _(pool):
            def scan(jb, jc, jd=None, ja=None, jn=None):
                if jb is None:
                    return
                if ja is not None:
                    fetch(0, ja)
                for s in range(NS):
                    h, n = s // N_STATE, s % N_STATE
                    pool.wait_ge(*hc_ok.at(jb, s + 1))
                    if n == 0:
                        g.tensor_tensor(sbm[:, 30:31], eps, eps, ALU.add).then_inc(*ysum.up())
                    else:
                        pool.wait_ge(*ysum.at(jb, s))
                        g.tensor_tensor(f(Y[h]), f(Y[h]), f(HC[n % 2]), ALU.add).then_inc(*ysum.up())
                    for unit, m in gather_share(s) if ja is not None else []:
                        if unit == "fetch":
                            fetch(m, ja)
                    if jn is not None and s in FETCH_AT:
                        fetch(FETCH_AT[s], jn)

            def fetch(m, ja):
                slot, before = places(ja).slot(m)
                h, b = groups[m]
                if m == 0:
                    pool.wait_ge(*index_ok.at(ja, 1))
                    pool.wait_ge(*table_in.at(ja, 16 * 32))
                pool.wait_ge(*pool_tick.at(ja, m))
                pool.wait_ge(*sample_ok.at(ja, max(before + 1, 0)))
                g.tensor_tensor(sa[:, 30:31], eps, eps, ALU.add).then_inc(*pool_tick.up())
                for k in range(TAPS):
                    g.indirect_dma_start(
                        out=slot[:, k, :, :].rearrange("p a c -> p (a c)"), out_offset=None, in_=tables[h],
                        in_offset=bass.IndirectOffsetOnAxis(ap=index[:, BLK * h + b, k:k + 1], axis=0),
                    ).then_inc(*gathered[m % SLOTS].up(16))

            def attention(jd, ja):
                if ja is not None:
                    if places(ja).ahead:
                        pool.wait_ge(*stu_ps.at(jd, 1))
                    for m in range(len(FETCH_AT) if places(ja).ahead else 0, GROUPS):
                        fetch(m, ja)

            pool.wait_ge(*ready.at(0, 1))
            run(pool, scan, attention)

        @block.scalar
        def _(act):
            exp_ln = lambda: a.preload_act_table_set("natural_log_exp_and_others")

            def setup():
                act.wait_ge(*mraw_in.at(0, 16 * RAW_LOADS))
                a.activation(spow[:], spow[:], ACT.Ln).then_inc(*boot_a.up())
                act.wait_ge(*boot_a.at(0, 1))
                a.activation(spow[:], spow[:], ACT.Exp, scale=0.25).then_inc(*boot_a.up())
                act.wait_ge(*boot_v.at(0, 3))
                a.activation(mixw[:, 12:16], mixw[:, 8:12], ACT.Exp).then_inc(*boot_a.up())
                act.wait_ge(*loaded.at(0, loaded.raised))
                act.wait_ge(*boot_v.at(0, 4))
                a.activation(negA[:], negA[:], ACT.Exp).then_inc(*boot_a.up())

            act.wait_ge(*ready.at(0, 1))
            exp_ln()

            def rstd_col(dst, src, i, ln, ok):
                a.activation(dst, src, ACT.Ln).then_inc(*ln.up())
                act.wait_ge(*ln.at(i, 1))
                a.activation(dst, dst, ACT.Exp, scale=-0.5).then_inc(*ok.up())

            def square(n, i):
                act.wait_ge(*n.cent.at(i, 1))
                a.activation(f(n.t1), f(n.t0), ACT.Square).then_inc(*n.sq.up())

            def rstd(n, i):
                act.wait_ge(*n.var.at(i, 1))
                a.activation(f(n.t1), n.p1[:], ACT.Ln, bias=eps).then_inc(*n.ln.up())
                act.wait_ge(*n.ln.at(i, 1))
                a.activation(f(n.t1), f(n.t1), ACT.Exp, scale=-0.5).then_inc(*n.rstd.up())

            def scan(jb, jc, jd=None, ja=None, jn=None):
                def inner(h):
                    act.wait_ge(*xz_ps.at(jb, 2 * h + 1))
                    a.activation(f(HC[h]), ps[2][:], ACT.Identity, bias=cb, scale=cw1).then_inc(*xh_pre.up())
                    act.wait_ge(*xz_ps.at(jb, 2 * h + 2))
                    a.activation(f(SZ[h]), ps[3][:], ACT.Silu)
                    act.wait_ge(*conv2.at(jb, h + 1))
                    a.activation(f(XC[h]), f(HC[h]), ACT.Silu).then_inc(*xc_ok.up())

                def rows(h):
                    act.wait_ge(*xdbl_ps.at(jb, 2 * h + 1))
                    a.copy(bcs[h], ps[2][0:96, :]).then_inc(*bc_hi.up())
                    act.wait_ge(*xdbl_ps.at(jb, 2 * h + 2))
                    a.copy(F[0:DT_RANK, Y[h], :], ps[3][0:DT_RANK, :]).then_inc(*dtlow_ok.up())

                def step(h):
                    act.wait_ge(*dtp_ps.at(jb, h + 1))
                    a.activation(f(DA[h]), ps[3][:], ACT.Abs, bias=bdt).then_inc(*sp_abs.up())
                    a.activation(f(DT[h]), ps[3][:], ACT.Relu, bias=bdt).then_inc(*dtp_read.up())

                if jc is not None:
                    square(lc1, jc)
                if jb is not None and jc is None:
                    act.wait_ge(*x1_ok.at(jb, 2))
                    a.copy(XF[:], xin[:]).then_inc(*xcopy_ok.up())
                if jb is not None:
                    inner(0)
                if jc is not None:
                    exp_ln()
                    rstd(lc1, jc)
                if jd is not None:
                    start(jd)
                if jb is not None:
                    rows(0)
                work(None, ja, [("norm", 0)])
                if jc is not None:
                    act.wait_ge(*lin_ps.at(jc, 1))
                    a.activation(f(UT), ps[0][:], ACT.Identity, bias=bk).then_inc(*lk_ok.up())
                if jb is not None:
                    step(0)
                work(None, ja, [("offsets", 0)])
                if jb is not None:
                    inner(1)
                work(None, ja, [("offsets", 1)])
                if jb is not None:
                    rows(1)
                if jc is not None:
                    square(lc2, jc)
                if jb is not None:
                    step(1)
                    if jc is not None:
                        act.wait_ge(*lc2.x.at(jc, 1))
                        a.copy(XF[:], xin[:]).then_inc(*xcopy_ok.up())
                    exp_ln()
                if jc is not None:
                    rstd(lc2, jc)
                if jb is not None:
                    for h in range(2):
                        act.wait_ge(*sp_abs.at(jb, h + 1))
                        a.activation(f(DA[h]), f(DA[h]), ACT.Exp, scale=-1.0).then_inc(*sp_exp.up())
                        act.wait_ge(*sp_exp.at(jb, h + 1))
                        a.activation(f(DBX[h]), f(DA[h]), ACT.Ln, bias=1.0).then_inc(*sp_ln.up())
                if jc is not None:
                    act.wait_ge(*lc2.ok.at(jc, 1))
                    pad = cpad(jc)[:]
                    for c in range(2):
                        last = a.copy(F[:, RING, HALF * c:HALF * c + HALF].rearrange("p (j s) -> p j s", j=4),
                                      bass.AP(pad.tensor, pad.offset + 2 + c + 2 * (P - 1), [[pad.ap[0][0], P], [2 * P, 4], [-2, P]]))
                    last.then_inc(*urev_ok.up())
                    act.wait_ge(*uT_ps.at(jc, 1))
                    a.copy(f(UT), ps[1][:]).then_inc(*uT_ok.up())
                for s in range(NS):
                    if jb is not None:
                        h, n = s // N_STATE, s % N_STATE
                        if s == 0:
                            act.wait_ge(*dtx_ok.at(jb, 2))
                        act.wait_ge(*dt_ok.at(jb, h + 1))
                        if s >= 2:
                            act.wait_ge(*scan_ok.at(jb, s - 1))
                        a.activation(f(DA[s % 2]), f(DT[h]), ACT.Exp, scale=negA[:, n:n + 1]).then_inc(*dA_ok.up())
                    if jc is not None:
                        m = 2 * s
                        act.wait_ge(*conv_ps.at(jc, m + 1))
                        if m >= 4:
                            act.wait_ge(*conv_used.at(jc, m - 3))
                        a.copy(ring[m % 4], ps[1][:, 0:HALF]).then_inc(*conv_a.up())
                    if jd is not None:
                        work(jd, None, share(s))
                    if ja is not None:
                        work(None, ja, gather_share(s))
                    if jn is not None:
                        front(s, jn)
                if ja is not None:
                    work(None, ja, gather_share(NS))
                if jb is not None:
                    act.wait_ge(*varB_ok.at(jb, 1))
                    rstd_col(sbm[:, 20:21], sbm[:, 19:20], jb, lnB_ok, rstdB_ok)
                    act.wait_ge(*aff_ok.at(jb, 1))
                    a.activation(f(HS), ps[2][:], ACT.Silu, bias=sbm[:, 22:23], scale=sbm[:, 21:22]).then_inc(*gns_ok.up())
                    exp_ln()
                if jc is not None:
                    square(ld1, jc)
                    rstd(ld1, jc)

            def start(jd):
                for n in range(3):
                    act.wait_ge(*qkv_ps.at(jd, n + 1))
                    a.copy(f((Q, K, V)[n]), ps[2 + n % 2][:]).then_inc(*qkv_ok.up())
                probabilities(0, jd)

            def probabilities(m, jd):
                n = P * (m % BLK + 1)
                act.wait_ge(*negmax.at(jd, m + 1))
                if m >= 2:
                    last_chunk = max(c for c, ch in enumerate(chunks) if ch[0] == m - 2)
                    act.wait_ge(*pT_ps.at(jd, last_chunk + 1))
                a.activation(F[:, PR[m % 2], 0:n], ps[2 + m % 2][:, 0:n], ACT.Exp, bias=sd[:, 2 * (m % 2):2 * (m % 2) + 1],
                             scale=SCORE_SCALE, accum_out=sd[:, 4 + m % 2:5 + m % 2]).then_inc(*probs.up())

            def chunk_copies(m, jd):
                for c, (j, b0, b1) in enumerate(chunks):
                    if j == m:
                        act.wait_ge(*pT_ps.at(jd, c + 1))
                        if c >= 4:
                            act.wait_ge(*pv_done.at(jd, c - 3))
                        a.copy(pts[c % 4][:, 0:P * (b1 - b0)], ps[2 + m % 2][:, HALF:HALF + P * (b1 - b0)]).then_inc(*pT_ok.up())

            def rstd_A(ja):
                act.wait_ge(*varA_ok.at(ja, 1))
                rstd_col(sa[:, 20:21], sa[:, 19:20], ja, lnA_ok, rstdA_ok)

            def copy_xnT(ja):
                act.wait_ge(*xnT_ps.at(ja, 1))
                a.copy(places(ja).xnT, places(ja).ps_xnT[:]).then_inc(*xnT_ok.up())

            def copy_offT(half, ja):
                act.wait_ge(*offT_ps.at(ja, half + 1))
                by_pixel = lambda ap: ap.rearrange("p (y x) -> p y x", x=W)[:, H // 2 * half:H // 2 * half + H // 2, :]
                offT, sums = by_pixel(places(ja).offT), by_pixel(places(ja).ps_offT[0:96, :])
                a.copy(offT[0:32, :, 1:W], sums[0:32, :, 0:W - 1])
                a.copy(offT[32:64], sums[32:64])
                a.copy(offT[64:96, :, 0:W - 1], sums[64:96, :, 1:W]).then_inc(*offT_ok.up())

            def front(s, ja):
                step = FRONT.get(s)
                if step == "average":
                    rstd_A(ja)
                if step == "turn x":
                    copy_xnT(ja)
                if step == "offsets 0":
                    copy_offT(0, ja)
                if step == "offsets 1":
                    copy_offT(1, ja)

            def samples_by_channel(m, ja):
                st = places(ja).st
                q, col = m // 4, P * (m % 4)
                act.wait_ge(*sample_ps.at(ja, m + 1))
                if q >= 2:
                    act.wait_ge(*conv_q.at(ja, q - 1))
                a.copy(st[q % 2][:, 0:4, col:col + P], bank_t0.rearrange("p (k q) -> p k q", q=P)).then_inc(*sampleT.up())
                if m % 4 == 3:
                    a.copy(st[q % 2][0:C, 4, :], bank_t1[0:C, :]).then_inc(*sampleT4.up())

            def work(jd, ja, units):
                for unit, m in units:
                    if unit == "norm" and ja is not None:
                        rstd_A(ja)
                        copy_xnT(ja)
                    if unit == "offsets" and ja is not None:
                        copy_offT(m, ja)
                    if unit == "turn" and ja is not None:
                        samples_by_channel(m, ja)
                    if unit == "query" and jd is not None:
                        chunk_copies(m, jd)
                    if unit == "values" and jd is not None and m + 1 < GROUPS:
                        probabilities(m + 1, jd)
                    if unit == "router" and m == 0 and jd is not None:
                        square(ld2, jd)
                        rstd(ld2, jd)
                    if unit == "router" and m == 2 and jd is not None:
                        act.wait_ge(*top_in.at(jd, 1))
                        a.activation(rtop[:, 2, :], rtop[:, 2, :], ACT.Exp).then_inc(*top_exp.up())
                    if unit == "expert" and m == GATES_AT and jd is not None:
                        act.wait_ge(*gateT_ps.at(jd, 1))
                        a.copy(F[0:2 * EXPERTS, Q, :], ps[2][0:2 * EXPERTS, :]).then_inc(*gateT_ok.up())

            def attention(jd, ja):
                if ja is not None and not places(ja).ahead:
                    work(None, ja, [("norm", 0), ("offsets", 0), ("offsets", 1)])
                if first_pair(ja):
                    setup()
                if jd is not None:
                    start(jd)
                work(jd, ja, attention_order(ja))
                if first_pair(ja):
                    act.wait_ge(*setup_done.at(0, 1))

            run(act, scan, attention)

        @block.tensor
        def _(pe):
            def mm(o, w, r, start=True, stop=True):
                return t.matmul(o, w, r, start=start, stop=stop)

            def add(o, w, r):
                return t.matmul(o, w, r, start=False, stop=False, skip_group_check=True)

            def wide(o, w, r, start=True, stop=True):
                for q in range(2):
                    s = slice(HALF * q, HALF * q + HALF)
                    last = mm(o[:, s], w, r[:, s], start, stop)
                return last

            def mean(n, i):
                pe.wait_ge(*n.x.at(i, 1))
                wide(n.p0, mean64, n.src(i)).then_inc(*n.mean.up())

            def variance(n, i):
                pe.wait_ge(*n.sq.at(i, 1))
                wide(n.p1, mean64, f(n.t1)).then_inc(*n.var.up())

            def scan(jb, jc, jd=None, ja=None, jn=None):
                source = XF if jc is None else xin

                def project(h):
                    if h == 0:
                        pe.wait_ge(*(xcopy_ok.at(jb, 1) if jc is None else x1_ok.at(jb, 2)))
                        if jc is not None and (not isinstance(jc, int) or jc > 0):
                            pe.wait_ge(*out_ok.at(jc - 1, 1))
                    else:
                        pe.wait_ge(*bc_ok.at(jb, 1))
                        pe.wait_ge(*dtp_read.at(jb, 1))
                    wide(ps[2], win[:, h, 0:P], source).then_inc(*xz_ps.up())
                    wide(ps[3], win[:, h, P:2 * P], source).then_inc(*xz_ps.up())

                def low_rank(h):
                    pe.wait_ge(*xc_ok.at(jb, h + 1))
                    wide(ps[2][0:96, :], wxbc[:], f(XC[h])).then_inc(*xdbl_ps.up())
                    wide(ps[3][0:DT_RANK, :], wxdt[:], f(XC[h])).then_inc(*xdbl_ps.up())

                def step_size(h):
                    pe.wait_ge(*dtlow_ok.at(jb, h + 1))
                    wide(ps[3], wdt[:], F[0:DT_RANK, Y[h], :]).then_inc(*dtp_ps.up())

                def linear(n, w, dst):
                    wide(dst, wqkv2[:, w, :], cpad(jc)[:, 2:]).then_inc(*lin_ps.up())

                if jc is not None:
                    if jb is not None:
                        pe.wait_ge(*x1_ok.at(jb, 2))
                    mean(lc1, jc)
                if jb is not None:
                    project(0)
                if jc is not None:
                    variance(lc1, jc)
                if jd is not None:
                    start(jd)
                if jb is not None:
                    low_rank(0)
                work(None, ja, [("norm", 0)])
                if jc is not None:
                    pe.wait_ge(*lc1.ok.at(jc, 1))
                    linear(0, 1, ps[0])
                if jb is not None:
                    step_size(0)
                work(None, ja, [("offsets", 0)])
                if jc is not None:
                    linear(1, 2, ps[1])
                if jb is not None:
                    project(1)
                work(None, ja, [("offsets", 1)])
                if jc is not None:
                    pe.wait_ge(*lk_ok.at(jc, 1))
                    linear(2, 0, ps[0])
                if jb is not None:
                    low_rank(1)
                work(None, ja, [("turn offsets", 0)])
                if jc is not None:
                    mean(lc2, jc)
                if jb is not None:
                    step_size(1)
                if jc is not None:
                    variance(lc2, jc)
                    pe.wait_ge(*urev_ok.at(jc, 1))
                    for n in range(BLK):
                        last = t.transpose(ps[1][:, P * n:P * n + P], F[:, RING, P * n:P * n + P], ident)
                    last.then_inc(*uT_ps.up())
                    xpar = late(jc)[:].rearrange("p (t a) -> p a t", a=2)
                    for ap in range(2):
                        mm(ps[0][:, HALF * ap:HALF * ap + HALF], ident, xpar[:, ap, :])
                    pe.wait_ge(*uT_ok.at(jc, 1))
                uT = f(UT).rearrange("p (n c) -> p n c", c=P)

                def convolve(m):
                    k, ap, odd = m // 4, m // 2 % 2, m % 2
                    src = ap ^ odd
                    lag = 1 if not (odd and ap == 0) else 0
                    if m % 4 == 0:
                        pe.wait_ge(*tiles_in[k % 2].at(jc, 48 * (k // 2 + 1)))
                    for j in range(4):
                        n = HALF - P * j
                        last = mm(ps[1][:, HALF * (m % 2) + P * j:HALF * (m % 2) + HALF], uT[:, 4 * src + j, :],
                                  toep[k % 2][:, odd, lag:lag + n], j == 0, j == 3)
                    last.then_inc(*conv_ps.up())

                def mix(m):
                    k, ap, odd = m // 4, m // 2 % 2, m % 2
                    pe.wait_ge(*(conv_a if m % 2 == 0 else conv_v).at(jc, m // 2 + 1))
                    for s0, s1, sg in SEGMENTS:
                        last = add(ps[0][:, HALF * ap + s0:HALF * ap + s1], mring[k % 2][:, 2 * sg + odd, :], ring[m % 4][:, s0:s1])
                    last.then_inc(*conv_used.up())

                def b_rows(s):
                    h, n = s // N_STATE, s % N_STATE
                    if s == 0:
                        pe.wait_ge(*bc_ok.at(jb, 2))
                    else:
                        pe.wait_ge(*bin_ok.at(jb, s))
                    wide(ps[2], sel[:, n, :], bcs[h]).then_inc(*b_ps.up())

                def c_rows(s):
                    h, n = s // N_STATE, s % N_STATE
                    if s == 0:
                        pe.wait_ge(*dtp_read.at(jb, 2))
                    else:
                        pe.wait_ge(*hc_ok.at(jb, s))
                    wide(ps[3], sel[:, N_STATE + n, :], bcs[h]).then_inc(*c_ps.up())

                if jb is not None:
                    b_rows(0)
                    c_rows(0)
                for s in range(NS):
                    if jc is not None:
                        convolve(2 * s)
                    step = FRONT.get(s) if jn is not None else None
                    if step:
                        pe.wait_ge(*bin_ok.at(jb, s + 1))
                        front(step, jn)
                    elif jb is not None and s + 1 < NS:
                        b_rows(s + 1)
                    if jd is not None:
                        work(jd, None, share(s)[:-1])
                    if jc is not None:
                        if s > 0:
                            mix(2 * s - 1)
                        convolve(2 * s + 1)
                    if step:
                        front_read(step, jn)
                        b_rows(s + 1)
                    if jb is not None and s + 1 < NS:
                        c_rows(s + 1)
                    if jd is not None:
                        work(jd, None, share(s)[-1:])
                    if jc is not None:
                        mix(2 * s)
                    if ja is not None:
                        work(None, ja, gather_share(s))
                if ja is not None:
                    work(None, ja, gather_share(NS))
                if jc is not None:
                    mix(2 * NS - 1)
                    for ap in range(2):
                        for s0, s1, sg in SEGMENTS:
                            for tap in range(3):
                                o = 2 + ap - tap + 2 * s0
                                last = add(ps[0][:, HALF * ap + s0:HALF * ap + s1], mar[:, sg, tap, :], cpad(jc)[:, o:o + 2 * (s1 - s0) - 1:2])
                    last.then_inc(*stu_ps.up())
                    mean(ld1, jc)
                if jb is not None:
                    pe.wait_ge(*y2_ok.at(jb, 2))
                    for q in range(2):
                        s = slice(HALF * q, HALF * q + HALF)
                        for h in range(2):
                            last = mm(ps[2][:, s], wout[:, h, :], F[:, Y[h], s], h == 0, h == 1)
                    last.then_inc(*mout_ps.up())
                    pe.wait_ge(*statB_in.at(jb, 1))
                    mm(ps[3][:, 0:2], mean16, sbm[:, 16:18]).then_inc(*statB_out.up())
                if jc is not None:
                    variance(ld1, jc)
                if jd is not None:
                    finish(jd)

            vtok = f(V).rearrange("p (n c) -> p n c", c=P)

            def scores(m, jd):
                r, qb = image[m // BLK], m % BLK
                if m >= 2:
                    pe.wait_ge(*ctx_ok.at(jd, m - 1))
                n = P * (qb + 1)
                for s0 in range(0, n, HALF):
                    s1 = min(n, s0 + HALF)
                    last = mm(ps[2 + m % 2][:, s0:s1], F[r, Q, P * qb:P * qb + P], F[r, K, s0:s1])
                last.then_inc(*score_ps.up())

            def turn(c, jd):
                j, b0, b1 = chunks[c]
                if b0 == 0:
                    pe.wait_ge(*probs.at(jd, j + 1))
                if c >= 1:
                    pe.wait_ge(*pT_ok.at(jd, c))
                for n in range(b0, b1):
                    last = t.transpose(ps[2 + j % 2][:, HALF + P * (n - b0):HALF + P * (n - b0) + P], F[:, PR[j % 2], P * n:P * n + P], ident)
                last.then_inc(*pT_ps.up())

            def values(c, jd):
                j, b0, b1 = chunks[c]
                h, qb = j // BLK, j % BLK
                pe.wait_ge(*pT_ok.at(jd, c + 1))
                for n in range(b0, b1):
                    last = mm(ps[2 + j % 2][:, 0:C], pts[c % 4][:, P * (n - b0):P * (n - b0) + P], vtok[:, n, C * h:C * h + C],
                              n == 0, n == qb)
                last.then_inc(*pv_done.up())

            def convolve_samples(q, ja):
                pe.wait_ge(*sampleT4.at(ja, q + 1))
                if q == 2:
                    pe.wait_ge(*x1_ok.at(ja, 1))
                st = places(ja).st
                for kk in range(KTILES):
                    n = P if kk < KTILES - 1 else C
                    last = mm(bank_conv, wmain[0:n, kk, q % 2, :], st[q % 2][0:n, kk, :],
                              q % 2 == 0 and kk == 0, q % 2 == 1 and kk == KTILES - 1)
                last.then_inc(*conv_q.up())

            def query(m, jd):
                if m + 1 < GROUPS:
                    scores(m + 1, jd)
                for c, (j, b0, b1) in enumerate(chunks):
                    if j == m:
                        turn(c, jd)

            def turn_samples(m, ja):
                pe.wait_ge(*sample_ok.at(ja, m + 1))
                if m == 0:
                    pe.wait_ge(*xnT_ok.at(ja, 1))
                else:
                    pe.wait_ge(*sampleT.at(ja, m))
                if m % 4 == 0 and m > 0:
                    pe.wait_ge(*sampleT4.at(ja, m // 4))
                sm = samples[m % 2][:].rearrange("p k c -> p (k c)")
                for kk in range(KTILES - 1):
                    t.transpose(bank_t0[:, P * kk:P * kk + P], sm[:, P * kk:P * kk + P], ident)
                t.transpose(bank_t1[0:C, P * (m % 4):P * (m % 4) + P], sm[:, P * 4:P * 4 + C], ident).then_inc(*sample_ps.up())
                if m >= 4 and m % 4 == 0:
                    convolve_samples(m // 4 - 1, ja)
                if m == GROUPS - 1:
                    convolve_samples(3, ja)

            def router(part, jd):
                if part == 0:
                    pe.wait_ge(*ctx_ok.at(jd, GROUPS))
                    for n in range(BLK):
                        last = t.transpose(ps[2][:, P * n:P * n + P], F[:, CTX, P * n:P * n + P], ident)
                    last.then_inc(*ctxT_ps.up())
                    mean(ld2, jd)
                    variance(ld2, jd)
                if part == 2:
                    pe.wait_ge(*ld2.ok.at(jd, 1))
                    for n in range(BLK):
                        last = mm(ps[2][:, 16 * n:16 * n + 16], upad[:, 2 + P * n:2 + P * n + P],
                                  wrouter[:].rearrange("p b e -> p (b e)"))
                    last.then_inc(*log_ps.up())

            def experts(m, jd):
                n, h = m // 2, m % 2
                r = image[h]
                if m >= 2:
                    pe.wait_ge(*exp_read.at(jd, m - 1))
                if m == GATES_AT:
                    gates = route[:, 8, :, :].rearrange("p g e -> p (g e)")
                    for b in range(BLK):
                        last = t.transpose(ps[2][0:16, P * b:P * b + P], gates[:, 16 * b:16 * b + 16], ident)
                    last.then_inc(*gateT_ps.up())
                mm(ps[3][:, HALF * h:HALF * h + HALF], upad[r, 2 + P * n:2 + P * n + P],
                   wexp[r, :, :].rearrange("p e c -> p (e c)")).then_inc(*exp_ps.up())

            def start(jd):
                pe.wait_ge(*ld1.ok.at(jd, 1))
                wide(ps[2], wqkv3[:, 0, :], upad[:, 2:]).then_inc(*qkv_ps.up())
                wide(ps[3], wqkv3[:, 1, :], upad[:, 2:]).then_inc(*qkv_ps.up())
                pe.wait_ge(*qkv_ok.at(jd, 1))
                for n in range(BLK):
                    last = mm(ps[2][:, P * n:P * n + P], upad[:, 2 + P * n:2 + P * n + P], wqkv3[:, 2, :])
                last.then_inc(*qkv_ps.up())
                pe.wait_ge(*qkv_ok.at(jd, 3))
                scores(0, jd)

            def average(ja):
                pe.wait_ge(*statA_in.at(ja, 1))
                mm(places(ja).ps_mean[:, 0:2], mean2, sa[:, 16:18]).then_inc(*statA_out.up())

            def turn_x(ja):
                pe.wait_ge(*xn_ok.at(ja, 1))
                for n in range(BLK):
                    tile = places(ja).xpad[:, 1 + 4 * n:5 + 4 * n, :].rearrange("p y x -> p (y x)")
                    last = t.transpose(places(ja).ps_xnT[:, P * n:P * n + P], tile, ident)
                last.then_inc(*xnT_ps.up())

            def offsets(half, ja):
                for dy in range(3):
                    rows = places(ja).xpad[:, H // 2 * half + dy:H // 2 * half + dy + H // 2, :].rearrange("p y x -> p (y x)")
                    last = mm(places(ja).ps_offT[0:96, HALF * half:HALF * half + HALF], woff[:, dy, :], rows, dy == 0, dy == 2)
                last.then_inc(*offT_ps.up())

            def front(step, ja):
                if step == "average":
                    average(ja)
                if step == "turn x":
                    turn_x(ja)
                if step == "offsets 0":
                    offsets(0, ja)
                if step == "offsets 1":
                    offsets(1, ja)
                if step == "turn offsets":
                    turn_offsets(ja)

            def front_read(step, ja):
                if step == "average":
                    pe.wait_ge(*varA_ok.at(ja, 1))
                if step == "turn x":
                    pe.wait_ge(*xnT_ok.at(ja, 1))
                if step == "offsets 0":
                    pe.wait_ge(*offT_ok.at(ja, 1))
                if step == "offsets 1":
                    pe.wait_ge(*offT_ok.at(ja, 2))
                if step == "turn offsets":
                    pe.wait_ge(*off_read.at(ja, 1))

            def turn_offsets(ja):
                pe.wait_ge(*offT_ok.at(ja, 2))
                for n in range(BLK):
                    last = mm(places(ja).ps_offs[:, 12 * n:12 * n + 12], places(ja).offT[:, P * n:P * n + P], pick[0:96, 0:12])
                last.then_inc(*off_ps.up())

            def work(jd, ja, units):
                for unit, m in units:
                    if unit == "norm" and ja is not None:
                        average(ja)
                        turn_x(ja)
                    if unit == "offsets" and ja is not None:
                        offsets(m, ja)
                    if unit == "turn offsets" and ja is not None:
                        turn_offsets(ja)
                    if unit == "turn" and ja is not None:
                        turn_samples(m, ja)
                    if unit == "query" and jd is not None:
                        query(m, jd)
                    if unit == "values" and jd is not None:
                        for c, (j, b0, b1) in enumerate(chunks):
                            if j == m:
                                values(c, jd)
                    if unit == "router" and jd is not None:
                        router(m, jd)
                    if unit == "expert" and jd is not None:
                        experts(m, jd)
            def finish(jd):
                pe.wait_ge(*gateT_ok.at(jd, 1))
                for n in range(BLK):
                    pe.wait_ge(*moe_ok.at(jd, 2 * n + 2))
                    s = slice(P * n, P * n + P)
                    mm(ps[2][:, s], bexp[:], F[0:2 * EXPERTS, Q, s], True, False)
                    last = mm(ps[2][:, s], F[:, MO, s], ident, False, True)
                last.then_inc(*moe_ps.up())

            def attention(jd, ja):
                if ja is not None and not places(ja).ahead:
                    work(None, ja, [("norm", 0), ("offsets", 0), ("offsets", 1), ("turn offsets", 0)])
                if first_pair(ja):
                    pe.wait_ge(*loaded.at(0, loaded.raised))
                if jd is not None:
                    start(jd)
                work(jd, ja, attention_order(ja))
                if jd is not None:
                    finish(jd)
                if first_pair(ja):
                    pe.wait_ge(*setup_done.at(0, 1))

            pe.wait_ge(*ready.at(0, 1))
            run(pe, scan, attention)

        @block.vector
        def _(dve):
            boot = lambda ins: (ins.then_inc(*boot_v.up()), dve.wait_ge(*boot_v.at(0, boot_v.raised)))
            based = [s for _, s in signals if s.base]
            for tile in (woff, wmain, win, wout, wqkv2, wqkv3, wrouter, bexp, mar, mring[0], mring[1]):
                last = v.memset(tile[:], 0.0)
                if based:
                    last.then_inc(based.pop().sem, 1)
            v.memset(eps, 1.0e-5)
            v.memset(upad[:, 0:2], 0.0).then_inc(*zeroed.up())
            dve.wait_ge(*early.at(0, early.raised))
            for h, r in enumerate(image):
                taps = woff[r].rearrange("p y (x c) -> p (y x) c", c=32)
                given = F[r, 16, 0:TAPS * 18].rearrange("p (k o) -> p k o", o=18)
                v.tensor_copy(taps[:, :, 6 * h:6 * h + 3], given[:, :, 0:18:6])
                v.tensor_copy(taps[:, :, 6 * h + 3:6 * h + 6], given[:, :, 1:6:2])
            v.memset(sa[:, 31:32], 0.0).then_inc(*ready.up())

            def setup():
                dve.wait_ge(*mraw_in.at(0, 16 * RAW_LOADS))
                mw = lambda n, k=4: mixw[:, n:n + k]
                boot(v.tensor_tensor(mw(8), mw(0), mw(4), ALU.add))
                boot(v.tensor_reduce(mw(16, 1), mw(8), AX.X, ALU.max))
                boot(v.tensor_scalar(mw(8), mw(8), mw(16, 1), None, ALU.subtract))
                dve.wait_ge(*loaded.at(0, loaded.raised))
                boot(v.tensor_scalar(negA[:], negA[:], 80.0, None, ALU.min))
                dve.wait_ge(*boot_a.at(0, 3))
                boot(v.tensor_reduce(mw(17, 1), mw(12), AX.X, ALU.add))
                boot(v.reciprocal(mw(18, 1), mw(17, 1)))
                boot(v.tensor_scalar(mw(20), mw(12), mw(18, 1), None, ALU.mult))
                boot(v.tensor_reduce(mw(19, 1), mw(20), AX.X, ALU.max))
                boot(v.tensor_scalar(mw(24), mw(20), mw(19, 1), None, ALU.is_ge))
                boot(v.tensor_tensor(mw(24), mw(24), rank[:, 4:8], ALU.mult))
                boot(v.tensor_reduce(mw(19, 1), mw(24), AX.X, ALU.max))
                boot(v.tensor_scalar(mw(24), mw(24), mw(19, 1), None, ALU.is_equal))
                boot(v.tensor_tensor(mw(24), mw(24), mw(20), ALU.subtract))
                boot(v.tensor_tensor(mw(24), mw(24), mw(20), ALU.add))
                flat = lambda n: F[0:C, n, :].rearrange("p (k e) -> p k e", e=C)
                sbc = spow[0:C, :].unsqueeze(2).broadcast_to([C, FILTERS, C])
                held = [F[0:C, 16, :], XF[0:C, :]]
                for e in range(STU_EXPERTS):
                    sg = 3 - e
                    if e == 2:
                        dve.wait_ge(*mixing_in.at(0, 16 * 4))
                    for odd in range(2):
                        n = held[odd].rearrange("p (k e) -> p k e", e=C)
                        boot(v.tensor_tensor(n, flat(e), flat(4 + e), ALU.subtract if odd else ALU.add))
                        boot(v.tensor_tensor(n, n, sbc, ALU.mult))
                        if e == 0:
                            boot(v.tensor_scalar(F[0:C, spec_tile(sg, odd), :], held[odd], mixw[0:C, 24:25], None, ALU.mult))
                        else:
                            boot(v.scalar_tensor_tensor(out=F[0:C, spec_tile(sg, odd), :], in0=held[odd], scalar=mixw[0:C, 24 + e:25 + e],
                                                        in1=F[0:C, spec_tile(sg + 1, odd), :],
                                                        op0=ALU.mult, op1=ALU.add))
                    v.memset(sbm[:, 31:32], 0.0).then_inc(*mspec_ok.up())
                    for r in image:
                        mu = F[r, 8, 3 * C * e:3 * C * e + 3 * C].rearrange("p (k e) -> p k e", e=C)
                        if e == 0:
                            boot(v.tensor_scalar(mar[r, sg, :, r], mu, mixw[r, 24:25], None, ALU.mult))
                        else:
                            boot(v.scalar_tensor_tensor(out=mar[r, sg, :, r], in0=mu, scalar=mixw[r, 24 + e:25 + e],
                                                        in1=mar[r, sg + 1, :, r], op0=ALU.mult, op1=ALU.add))
                dve.wait_ge(*boot_a.at(0, 4))
                v.tensor_scalar(negA[:], negA[:], -1.0, None, ALU.mult)
                v.tensor_copy(sel[:], pick[0:96, :].unsqueeze(2).broadcast_to([96, 32, P])).then_inc(*setup_done.up())

            def link(ins, s, i):
                ins.then_inc(*s.up())
                dve.wait_ge(*s.at(i, (s.raised - 1) % s.per_pair + 1))

            def channel_stats(src, small, s, i, stat_in):
                for q in range(2):
                    ins = v.bn_stats(small[:, 6 * q:6 * q + 6], src[:, HALF * q:HALF * q + HALF])
                link(ins, s, i)
                v.tensor_copy(small[:, 28:29], eps)
                link(v.bn_aggr(small[:, 16:18], small[:, 0:12].rearrange("p (a b) -> p a b", a=2)), s, i)
                v.scalar_tensor_tensor(out=small[:, 17:18], in0=small[:, 16:17], scalar=small[:, 16:17], in1=small[:, 17:18],
                                       op0=ALU.mult, op1=ALU.add).then_inc(*stat_in.up())

            def group_variance(small, s, i, stat_out, psum, var_ok):
                dve.wait_ge(*stat_out.at(i, 1))
                link(v.tensor_copy(small[:, 24:26], psum), s, i)
                link(v.scalar_tensor_tensor(out=small[:, 18:19], in0=small[:, 24:25], scalar=small[:, 24:25],
                                            in1=small[:, 25:26], op0=ALU.mult, op1=ALU.subtract), s, i)
                v.tensor_scalar(small[:, 19:20], small[:, 18:19], -1.0, 1.0e-5, ALU.mult, ALU.add).then_inc(*var_ok.up())

            def center(n, i):
                dve.wait_ge(*n.mean.at(i, 1))
                v.tensor_tensor(f(n.t0), n.src(i)[:], n.p0[:], ALU.subtract).then_inc(*n.cent.up())

            def normalise(n, i):
                dve.wait_ge(*n.rstd.at(i, 1))
                v.tensor_tensor(n.dst(i)[:, 2:], f(n.t0), f(n.t1), ALU.mult).then_inc(*n.ok.up())

            def scan(jb, jc, jd=None, ja=None, jn=None):
                def causal_conv(h):
                    dve.wait_ge(*xh_pre.at(jb, h + 1))
                    v.scalar_tensor_tensor(out=F[:, HC[h], 1:], in0=ps[2][:, 0:L - 1], scalar=cw0, in1=F[:, HC[h], 1:],
                                           op0=ALU.mult, op1=ALU.add).then_inc(*conv2.up())

                def split_rows(h):
                    rest = F[0:C, HS, :]
                    dve.wait_ge(*bc_hi.at(jb, h + 1))
                    link(v.tensor_tensor(rest, ps[2][0:C, :], bcs[h][0:C, :], ALU.subtract), vB, jb)
                    link(v.tensor_copy(bcs[h][0:C, :], rest), vB, jb)
                    v.tensor_tensor(bcs[h][0:32, :], rest[0:32, :], bcs[h][0:32, :], ALU.subtract).then_inc(*bc_ok.up())
                    dve.wait_ge(*bc_ok.at(jb, h + 1))

                def step_sizes(h):
                    dve.wait_ge(*sp_exp.at(jb, h + 1))
                    link(v.tensor_scalar(f(DTX[h]), f(DA[h]), 1.0, 1.0, ALU.add, ALU.subtract), vB, jb)
                    link(v.tensor_tensor(f(DTX[h]), f(DA[h]), f(DTX[h]), ALU.subtract), vB, jb)
                    dve.wait_ge(*dtp_read.at(jb, h + 1))
                    link(v.tensor_tensor(f(DT[h]), f(DT[h]), f(DTX[h]), ALU.add), vB, jb)
                    dve.wait_ge(*sp_ln.at(jb, h + 1))
                    v.tensor_tensor(f(DT[h]), f(DT[h]), f(DBX[h]), ALU.add).then_inc(*dt_ok.up())
                    dve.wait_ge(*dt_ok.at(jb, h + 1))
                    v.tensor_tensor(f(DTX[h]), f(DT[h]), f(XC[h]), ALU.mult).then_inc(*dtx_ok.up())

                if last_pair(jc):
                    v.memset(cpad(jc)[:, 0:2], 0.0)
                if jd is not None:
                    normalise(ld1, jd)
                if jc is not None:
                    center(lc1, jc)
                if jb is not None:
                    causal_conv(0)
                if jc is not None:
                    normalise(lc1, jc)
                if jd is not None:
                    row_max(0, jd)
                if jb is not None:
                    dve.wait_ge(*stored.at(jb, 0) if jc is None else stored.at(jc, 0))
                    split_rows(0)
                work(None, ja, [("norm", 0)])
                if jc is not None:
                    dve.wait_ge(*lin_ps.at(jc, 2))
                    dve.wait_ge(*lk_ok.at(jc, 1))
                    link(v.scalar_tensor_tensor(out=f(KV), in0=ps[1][:], scalar=bv, in1=f(UT), op0=ALU.add, op1=ALU.mult,
                                                accum_out=sd[:, 8:9]), vC, jc)
                if jb is not None:
                    causal_conv(1)
                if jc is not None:
                    dve.wait_ge(*lin_ps.at(jc, 3))
                    link(v.tensor_scalar(f(KV), ps[0][:], bq, sd[:, 8:9], ALU.add, ALU.mult), vC, jc)
                    v.tensor_tensor(late(jc)[:], XF[:], f(KV), ALU.add).then_inc(*lc2.x.up())
                if jb is not None:
                    split_rows(1)
                if jc is not None:
                    center(lc2, jc)
                    normalise(lc2, jc)
                work(None, ja, [("positions", 0)])
                if jb is not None:
                    step_sizes(0)
                    step_sizes(1)
                    dve.wait_ge(*dtx_ok.at(jb, 2))

                def input_term(s):
                    dve.wait_ge(*b_ps.at(jb, s + 1))
                    v.tensor_tensor(f(DBX[s % 2]), f(DTX[s // N_STATE]), ps[2][:], ALU.mult).then_inc(*bin_ok.up())

                def finish_y(h):
                    dve.wait_ge(*ysum.at(jb, N_STATE * (h + 1)))
                    link(v.scalar_tensor_tensor(out=f(Y[h]), in0=f(XC[h]), scalar=dskip, in1=f(Y[h]), op0=ALU.mult, op1=ALU.add), vB, jb)
                    v.tensor_tensor(f(Y[h]), f(Y[h]), f(SZ[h]), ALU.mult).then_inc(*y2_ok.up())

                if jb is not None:
                    input_term(0)
                for s in range(NS):
                    if jb is not None:
                        h, n = s // N_STATE, s % N_STATE
                        dve.wait_ge(*dA_ok.at(jb, s + 1))
                        dve.wait_ge(*bin_ok.at(jb, s + 1))
                        if s >= 1:
                            dve.wait_ge(*hc_ok.at(jb, s))
                        v.tensor_tensor_scan(f(HS), f(DA[s % 2]), f(DBX[s % 2]), 0.0, ALU.mult, ALU.add).then_inc(*scan_ok.up())
                        step = FRONT.get(s) if jn is not None else None
                        if step == "average":
                            variance(jn)
                        if step == "turn offsets":
                            positions(jn, [0])
                        if s + 1 < NS and not step:
                            input_term(s + 1)
                        dve.wait_ge(*scan_ok.at(jb, s + 1))
                        dve.wait_ge(*c_ps.at(jb, s + 1))
                        if s >= 2:
                            dve.wait_ge(*ysum.at(jb, s - 1))
                        v.tensor_tensor(f(Y[h]) if n == 0 else f(HC[n % 2]), f(HS), ps[3][:], ALU.mult).then_inc(*hc_ok.up())
                        if step:
                            input_term(s + 1)
                        if s == N_STATE + 2:
                            finish_y(0)
                    if jd is not None:
                        work(jd, None, share(s))
                    if jc is not None:
                        m = 2 * s + 1
                        dve.wait_ge(*conv_ps.at(jc, m + 1))
                        if m >= 4:
                            dve.wait_ge(*conv_used.at(jc, m - 3))
                        v.tensor_copy(ring[m % 4], ps[1][:, HALF:L]).then_inc(*conv_v.up())
                    if ja is not None:
                        work(None, ja, gather_share(s))
                    if jn is not None:
                        if step == "stats":
                            stats(jn)
                        if step == "shift":
                            shift(jn)
                        if 9 <= s < 8 + POSITION_PARTS:
                            positions(jn, [s - 8])
                        if s in GATHER_AT:
                            interpolate(GATHER_AT[s], jn)
                if jb is not None:
                    finish_y(1)
                if ja is not None:
                    work(None, ja, gather_share(NS))
                    v.memset(upad[:, 0:2], 0.0)
                    v.memset(lent[:, 2 * L + 2:], 0.0).then_inc(*cleared.up())
                if jc is not None:
                    dve.wait_ge(*stu_ps.at(jc, 1))
                    v.tensor_copy(late(jc)[:].rearrange("p (t a) -> p a t", a=2), ps[0][:].rearrange("p (a t) -> p a t", a=2)).then_inc(*ld1.x.up())
                if jb is not None:
                    dve.wait_ge(*mout_ps.at(jb, 1))
                    channel_stats(ps[2], sbm, vB, jb, statB_in)
                    group_variance(sbm, vB, jb, statB_out, ps[3][:, 0:2], varB_ok)
                    dve.wait_ge(*rstdB_ok.at(jb, 1))
                    link(v.tensor_tensor(sbm[:, 21:22], sbm[:, 20:21], gamma, ALU.mult), vB, jb)
                    link(v.tensor_tensor(sbm[:, 23:24], sbm[:, 24:25], sbm[:, 21:22], ALU.mult), vB, jb)
                    v.tensor_tensor(sbm[:, 22:23], beta, sbm[:, 23:24], ALU.subtract).then_inc(*aff_ok.up())
                if jc is not None:
                    center(ld1, jc)
                if jd is not None:
                    finish(jd)
                if jb is not None:
                    dve.wait_ge(*gns_ok.at(jb, 1))
                    v.tensor_tensor(XF[:], XF[:], f(HS), ALU.add).then_inc(*lc1.x.up())

            def stats(ja):
                dve.wait_ge(*xin_in.at(ja, 16))
                channel_stats(xin, sa, vA, ja, statA_in)

            def variance(ja):
                group_variance(sa, vA, ja, statA_out, places(ja).ps_mean[:, 0:2], varA_ok)

            def shift(ja):
                xpad = places(ja).xpad
                dve.wait_ge(*rstdA_ok.at(ja, 1))
                v.memset(xpad[:, 0:1, :], 0.0)
                v.memset(xpad[:, H + 1:H + 2, :], 0.0)
                v.memset(places(ja).offT[0:32, 0:L:W], 0.0)
                v.memset(places(ja).offT[64:96, W - 1:L:W], 0.0)
                v.tensor_scalar(xpad[:, 1:1 + H, :], xin[:].rearrange("p (y x) -> p y x", y=H), sa[:, 24:25],
                                sa[:, 20:21], ALU.subtract, ALU.mult).then_inc(*xn_ok.up())

            def positions(i, parts=range(POSITION_PARTS)):
                cd = lambda n: coord[:, n, :]
                cg = lambda n: coord[:, n, :].rearrange("p (g a k) -> p g a k", g=GROUPS, a=2)
                if 0 in parts:
                    dve.wait_ge(*off_ps.at(i, 1))
                    raw = places(i).ps_offs[:, 0:96].rearrange("p (n b o) -> p n b o", n=BLK, b=2)
                    for b in range(2):
                        for axis, bias in ((0, boff[:, 0:18:6]), (1, boff[:, 1:6:2])):
                            ins = v.tensor_tensor(cg(0)[:, BLK * b:BLK * b + BLK, axis, :], raw[:, :, b, 3 * axis:3 * axis + 3],
                                                  bias.unsqueeze(1).broadcast_to([P, BLK, 3]), ALU.add)
                    ins.then_inc(*off_read.up())
                    dve.wait_ge(*off_read.at(i, 1))
                if 1 in parts:
                    link(v.tensor_tensor(cg(0)[:, :, :, 1], cg(0)[:, :, :, 1], cg(0)[:, :, :, 0], ALU.add), vA, i)
                    link(v.tensor_tensor(cg(0)[:, :, :, 2], cg(0)[:, :, :, 2], cg(0)[:, :, :, 1], ALU.add), vA, i)
                    link(v.tensor_tensor(cd(1), cd(0), base, ALU.add), vA, i)
                    link(v.tensor_scalar(cd(1), cd(1), 1.0, W * 0.5, ALU.add, ALU.mult), vA, i)
                if 2 in parts:
                    link(v.tensor_scalar(cd(1), cd(1), 0.5, -2.0, ALU.subtract, ALU.max), vA, i)
                    link(v.tensor_scalar(cd(1), cd(1), float(W + 1), None, ALU.min), vA, i)
                    link(v.tensor_copy(cd(2).bitcast(I32), cd(1)), vA, i)
                    link(v.tensor_copy(cd(3), cd(2).bitcast(I32)), vA, i)
                if 3 in parts:
                    link(v.tensor_tensor(cd(4), cd(3), cd(1), ALU.is_gt), vA, i)
                    link(v.tensor_tensor(cd(5), cd(3), cd(4), ALU.subtract), vA, i)
                    ws = wsplit[:].rearrange("p g a k s -> p (g a k) s")
                    link(v.tensor_tensor(ws[:, :, 1], cd(1), cd(5), ALU.subtract), vA, i)
                    v.tensor_scalar(ws[:, :, 0], ws[:, :, 1], -1.0, 1.0, ALU.mult, ALU.add)
                    link(v.tensor_scalar(cg(6)[:, :, 1, :], cg(5)[:, :, 1, :], float(SIDE), float(2 * SIDE + 2), ALU.mult, ALU.add), vA, i)
                if 4 in parts:
                    v.tensor_tensor(index[:].rearrange("p g (x y) -> p g x y", x=3), cg(5)[:, :, 0, :].unsqueeze(3).broadcast_to([P, GROUPS, 3, 3]),
                                    cg(6)[:, :, 1, :].unsqueeze(2).broadcast_to([P, GROUPS, 3, 3]), ALU.add).then_inc(*index_ok.up())
                for k in range(CORNERS):
                    if 4 + k // 2 in parts:
                        ins = v.tensor_tensor(cweight[:, :, k, :].rearrange("p g (x y) -> p g x y", x=3),
                                              wsplit[:, :, 0, :, k % 2].unsqueeze(3).broadcast_to([P, GROUPS, 3, 3]),
                                              wsplit[:, :, 1, :, k // 2].unsqueeze(2).broadcast_to([P, GROUPS, 3, 3]), ALU.mult)
                if 5 in parts:
                    link(ins, vA, i)

            def interpolate(m, i):
                h, b = groups[m]
                s, _ = places(i).slot(m)
                dve.wait_ge(*gathered[m % SLOTS].at(i, 16 * TAPS * (m // SLOTS + 1)))
                wb = cweight[:, BLK * h + b, :, :].rearrange("p a k -> p k a").unsqueeze(3).broadcast_to([P, TAPS, CORNERS, C])
                link(v.tensor_tensor(s[:], s[:], wb, ALU.mult), vA, i)
                link(v.tensor_tensor(s[:, :, 0:2, :], s[:, :, 0:2, :], s[:, :, 2:4, :], ALU.add), vA, i)
                if m >= 2:
                    dve.wait_ge(*sample_ps.at(i, m - 1))
                v.tensor_tensor(samples[m % 2][:], s[:, :, 0, :], s[:, :, 1, :], ALU.add).then_inc(*sample_ok.up())

            def add_conv(tq, i):
                dve.wait_ge(*conv_q.at(i, 2 * tq + 2))
                half = xin[:, HALF * tq:HALF * tq + HALF]
                v.scalar_tensor_tensor(out=half, in0=bank_conv, scalar=bmain, in1=half, op0=ALU.add, op1=ALU.add).then_inc(*x1_ok.up())

            def row_max(m, jd):
                n = P * (m % BLK + 1)
                sc = ps[2 + m % 2]
                nm = 2 * (m % 2)
                dve.wait_ge(*score_ps.at(jd, m + 1))
                link(v.tensor_tensor(sc[:, n - P:n], sc[:, n - P:n], mask, ALU.add), vD, jd)
                link(v.tensor_reduce(sd[:, nm + 1:nm + 2], sc[:, 0:n], AX.X, ALU.max), vD, jd)
                v.tensor_scalar(sd[:, nm:nm + 1], sd[:, nm + 1:nm + 2], -SCORE_SCALE, None, ALU.mult).then_inc(*negmax.up())

            def context(j, jd):
                h, qb = j // BLK, j % BLK
                last_chunk = max(c for c, ch in enumerate(chunks) if ch[0] == j)
                dve.wait_ge(*pv_done.at(jd, last_chunk + 1))
                link(v.reciprocal(sd[:, 6 + j % 2:7 + j % 2], sd[:, 4 + j % 2:5 + j % 2]), vD, jd)
                v.tensor_scalar(F[:, CTX, P * qb + C * h:P * qb + C * h + C], ps[2 + j % 2][:, 0:C], sd[:, 6 + j % 2:7 + j % 2],
                                None, ALU.mult).then_inc(*ctx_ok.up())

            mo = f(MO).rearrange("p (n b c) -> p n b c", n=BLK, b=2)

            def router(part, jd):
                if part == 0:
                    context(GROUPS - 1, jd)
                    dve.wait_ge(*ctxT_ps.at(jd, 1))
                    v.tensor_tensor(late(jd)[:], late(jd)[:], ps[2][:], ALU.add).then_inc(*ld2.x.up())
                    center(ld2, jd)
                if part == 1:
                    normalise(ld2, jd)
                if part == 2:
                    dve.wait_ge(*log_ps.at(jd, 1))
                    rt = lambda n: route[:, n, :, :]
                    top = lambda n: rtop[:, n, :]
                    wide8 = lambda ap: ap.unsqueeze(2).broadcast_to([P, GROUPS, EXPERTS])
                    perg = lambda ap: ap.unsqueeze(1).broadcast_to([P, GROUPS, EXPERTS])
                    step = lambda ins: link(ins, vD, jd)
                    step(v.tensor_tensor(rt(0), ps[2][:, 0:P].rearrange("p (g e) -> p g e", e=EXPERTS), perg(brouter[:]), ALU.add))
                    for r in range(2):
                        lg = rt(0) if r == 0 else rt(4)
                        step(v.tensor_reduce(top(r), lg, AX.X, ALU.max))
                        step(v.tensor_tensor(rt(1), lg, wide8(top(r)), ALU.is_ge))
                        step(v.tensor_tensor(rt(1), rt(1), perg(rank), ALU.mult))
                        step(v.tensor_reduce(top(3), rt(1), AX.X, ALU.max))
                        step(v.tensor_tensor(rt(2 + r), rt(1), wide8(top(3)), ALU.is_equal))
                        if r == 0:
                            step(v.tensor_scalar(rt(5), rt(2), -1.0e30, None, ALU.mult))
                            step(v.tensor_tensor(rt(4), rt(0), rt(5), ALU.add))
                    v.tensor_tensor(top(2), top(1), top(0), ALU.subtract).then_inc(*top_in.up())
                    dve.wait_ge(*top_exp.at(jd, 1))
                    step(v.tensor_scalar(top(4), top(2), 1.0, None, ALU.add))
                    step(v.reciprocal(top(4), top(4)))
                    step(v.tensor_tensor(top(5), top(4), top(2), ALU.mult))
                    step(v.tensor_tensor(rt(6), rt(2), wide8(top(4)), ALU.mult))
                    step(v.tensor_tensor(rt(7), rt(3), wide8(top(5)), ALU.mult))
                    v.tensor_tensor(rt(8), rt(6), rt(7), ALU.add).then_inc(*gate_ok.up())
                    dve.wait_ge(*gate_ok.at(jd, 1))

            def experts(m, jd):
                n, h = m // 2, m % 2
                dve.wait_ge(*exp_ps.at(jd, m + 1))
                if m >= 2:
                    dve.wait_ge(*moe_ok.at(jd, m - 1))
                tmp = F[:, TMP + h, 0:HALF].rearrange("p (e c) -> p e c", c=C)
                v.tensor_tensor(tmp, ps[3][:, HALF * h:HALF * h + HALF].rearrange("p (e c) -> p e c", c=C),
                                route[:, 8, m, :].unsqueeze(2).broadcast_to([P, EXPERTS, C]), ALU.mult).then_inc(*exp_read.up())
                dve.wait_ge(*exp_read.at(jd, m + 1))
                v.tensor_reduce(mo[:, n, h, :], tmp.rearrange("p e c -> p c e"), AX.X, ALU.add).then_inc(*moe_ok.up())

            def work(jd, ja, units):
                for unit, m in units:
                    if unit == "norm" and ja is not None:
                        stats(ja)
                        variance(ja)
                        shift(ja)
                    if unit == "positions" and ja is not None:
                        positions(ja)
                    if unit == "gather" and ja is not None:
                        if first_pair(ja) and m == SETUP_AT:
                            setup()
                        interpolate(m, ja)
                    if unit == "turn" and ja is not None:
                        if m == 10:
                            add_conv(0, ja)
                        if m == GROUPS - 1:
                            add_conv(1, ja)
                    if unit == "query" and jd is not None and m >= 1:
                        context(m - 1, jd)
                    if unit == "values" and jd is not None and m + 1 < GROUPS:
                        row_max(m + 1, jd)
                    if unit == "router" and jd is not None:
                        router(m, jd)
                    if unit == "expert" and jd is not None:
                        experts(m, jd)

            def finish(jd):
                dve.wait_ge(*moe_ps.at(jd, 1))
                if last_pair(jd):
                    dve.wait_ge(*stored.at(jd, 0))
                v.tensor_tensor(f(OUT), late(jd)[:], ps[2][:], ALU.add).then_inc(*out_ok.up())

            def attention(jd, ja):
                whole = ja is not None and not places(ja).ahead
                if whole:
                    work(None, ja, [("norm", 0)])
                if jd is not None:
                    normalise(ld1, jd)
                if whole:
                    work(None, ja, [("positions", 0)])

                if jd is not None:
                    row_max(0, jd)
                work(jd, ja, attention_order(ja))
                if jd is not None:
                    finish(jd)

            run(dve, scan, attention)
            for name, s, times in (("STEPS_A", vA, 3), ("STEPS_B", vB, 3), ("STEPS_C", vC, 3), ("STEPS_D", vD, 3)):
                assert s.raised == s.per_pair * times, f"{name} = {s.raised // times} ({s.raised} in {times})"


def arrays_of(i):
    n = {k: np.asarray(w) for k, w in i.items()}
    phi = n["L2_ffn_phi"][:L]
    phi_pad = np.zeros((FILTERS, 2, P + HALF), phi.dtype)
    phi_pad[:, 0, P:] = phi[0::2].T
    phi_pad[:, 1, P:] = phi[1::2].T
    return {
        "x": n["x"], "consts": shape_constants(),
        "w_off": n["L0_conv_w_off"].transpose(1, 2, 3, 0).reshape(C, TAPS, 18), "b_off": n["L0_conv_b_off"],
        "w_main": n["L0_conv_w_main"].reshape(C, C, TAPS).transpose(2, 1, 0), "b_main": n["L0_conv_b_main"],
        "W_in": n["L1_conv_W_in"], "conv_w": n["L1_conv_conv_w"], "conv_b": n["L1_conv_conv_b"],
        "W_x": n["L1_conv_W_x"], "W_dt": n["L1_conv_W_dt"], "b_dt": n["L1_conv_b_dt"],
        "A_log": n["L1_conv_A_log"], "D": n["L1_conv_D"], "W_out": n["L1_conv_W_out"],
        "gn_gamma": n["L1_conv_gn_gamma"], "gn_beta": n["L1_conv_gn_beta"],
        "Wq2": n["L2_attn_Wq"], "bq2": n["L2_attn_bq"], "Wk2": n["L2_attn_Wk"], "bk2": n["L2_attn_bk"],
        "Wv2": n["L2_attn_Wv"], "bv2": n["L2_attn_bv"], "sigma": n["L2_ffn_sigma"], "phi_pad": phi_pad,
        "M_u": n["L2_ffn_M_u"], "M_plus": n["L2_ffn_M_phi_plus"], "M_minus": n["L2_ffn_M_phi_minus"],
        "log_weights": n["L2_ffn_log_weights"], "gumbel": n["L2_ffn_gumbel"],
        "Wq3": n["L3_attn_Wq"], "Wk3": n["L3_attn_Wk"], "Wv3": n["L3_attn_Wv"],
        "router_w": n["L3_ffn_router_w"], "router_b": n["L3_ffn_router_b"],
        "expert_w": n["L3_ffn_expert_w"], "expert_b": n["L3_ffn_expert_b"],
    }


def build(nc, arrays):
    args = [nc.dram_tensor(f"in_{k}_dram", w.shape, mybir.dt.from_np(w.dtype), kind="ExternalInput").ap()
            for k, w in arrays.items()]
    tables = [nc.dram_tensor(f"corners{n}", [SIDE * SIDE, CORNERS * C], F32).ap() for n in range(2)]
    out = nc.dram_tensor("out_0_dram", [BATCH, C, H, W], F32, kind="ExternalOutput").ap()
    nc.disable_value_cache = True
    mixing = nc.dram_tensor("mixing", [FILTERS, C, 8, C], F32).ap()
    hybrid_kernel(nc, *args, tables, mixing, out)


def kernel(**inputs):
    import concourse.bacc as bacc
    from concourse.bass_utils import run_bass_kernel_spmd

    arrays = {k: np.ascontiguousarray(w) for k, w in arrays_of(inputs).items()}
    nc = bacc.Bacc("TRN2", target_bir_lowering=False, num_devices=1)
    build(nc, arrays)
    r = run_bass_kernel_spmd(nc, [{f"in_{k}_dram": w for k, w in arrays.items()}], core_ids=[0])
    return r.results[0]["out_0_dram"]
```
